# Optimizing a Trainium2 kernel written in Bass

```python
import numpy as np
import jax
import jax.numpy as jnp

def _softmax(x, axis=-1):
    return jax.nn.softmax(x, axis=axis)

def _gelu(x):
    return jax.nn.gelu(x, approximate=True)

def _silu(x):
    return jax.nn.silu(x)

def _sigmoid(x):
    return jax.nn.sigmoid(x)

def _layernorm(x, axis=-1, eps=1e-05):
    m = jnp.mean(x, axis=axis, keepdims=True)
    v = jnp.var(x, axis=axis, keepdims=True)
    return (x - m) / jnp.sqrt(v + eps)

def _scatter_add(tgt, idx, src, axis=0):
    return tgt.at[idx].add(src)

def _segment_sum(src, seg, n):
    return jax.ops.segment_sum(src, seg, n)
kernel_name = 'mk_gnn_preln_d1_gnn_r8_b2b481'

def setup_inputs(seed: int=0):
    np.random.seed(seed)
    _w = jnp.asarray

    def _rec_inputs():
        import jax
        import jax.numpy as jnp
        _gk = jax.random.key(seed)
        x = -0.000202 + 1 * jax.random.normal(jax.random.fold_in(_gk, 1), (6250, 128), jnp.float32)
        src = jax.random.randint(jax.random.fold_in(_gk, 2), (200000,), 0, 6250, jnp.int32)
        dst = jnp.minimum((6250 * jax.random.uniform(jax.random.fold_in(_gk, 3), (200000,)) ** 2.0).astype(jnp.int32), 49999)
        _o = jnp.argsort(dst, stable=True)
        src = src[_o]
        dst = dst[_o]
        return (x, src, dst)
    x, src, dst = _rec_inputs()

    def _L0_gnn_setup():
        import jax, jax.numpy as jnp
        import numpy as np
        N = 6250
        DEG = 16
        DIM = 128
        H = 128

        def _lstm_last(seq, w_ih, w_hh, b):
            n = seq.shape[0]
            h_dim = w_hh.shape[1]
            h0 = jnp.zeros((n, h_dim), seq.dtype)

            def step(carry, x_t):
                h, c = carry
                gates = x_t @ w_ih.T + h @ w_hh.T + b
                i, f, g, o = jnp.split(gates, 4, axis=-1)
                c = jax.nn.sigmoid(f) * c + jax.nn.sigmoid(i) * jnp.tanh(g)
                h = jax.nn.sigmoid(o) * jnp.tanh(c)
                return ((h, c), None)
            (h, _), _ = jax.lax.scan(step, (h0, h0), jnp.swapaxes(seq, 0, 1))
            return h
        key = jax.random.key(seed)
        ks = jax.random.split(key, 8)
        x = jax.random.normal(ks[0], (N, DIM), dtype=jnp.float32)
        row = jnp.repeat(jnp.arange(N), DEG)
        col = jax.random.randint(ks[1], (N * DEG,), 0, N)
        edge_index = jnp.stack([row, col]).astype(jnp.int32)
        s = 1.0 / np.sqrt(H)
        w_ih = jax.random.uniform(ks[2], (4 * H, DIM), jnp.float32, -s, s)
        w_hh = jax.random.uniform(ks[3], (4 * H, H), jnp.float32, -s, s)
        b_ih = jax.random.uniform(ks[4], (4 * H,), jnp.float32, -s, s)
        b_hh = jax.random.uniform(ks[5], (4 * H,), jnp.float32, -s, s)
        w_lin = jax.random.uniform(ks[6], (H, H), jnp.float32, -s, s)
        b_lin = jax.random.uniform(ks[7], (H,), jnp.float32, -s, s)
        return {'x': x, 'edge_index': edge_index, 'w_ih': w_ih, 'w_hh': w_hh, 'b_ih': b_ih, 'b_hh': b_hh, 'w_lin': w_lin, 'b_lin': b_lin}
    _L0_gnn_all = _L0_gnn_setup()
    _L0_gnn_in = {k: v for k, v in _L0_gnn_all.items() if k in ('w_ih', 'w_hh', 'b_ih', 'b_hh', 'w_lin', 'b_lin')}
    del _L0_gnn_all
    return {'x': x, 'src': src, 'dst': dst, 'L0_gnn_w_ih': _L0_gnn_in['w_ih'], 'L0_gnn_w_hh': _L0_gnn_in['w_hh'], 'L0_gnn_b_ih': _L0_gnn_in['b_ih'], 'L0_gnn_b_hh': _L0_gnn_in['b_hh'], 'L0_gnn_w_lin': _L0_gnn_in['w_lin'], 'L0_gnn_b_lin': _L0_gnn_in['b_lin']}

def reference(x, src, dst, L0_gnn_w_ih, L0_gnn_w_hh, L0_gnn_b_ih, L0_gnn_b_hh, L0_gnn_w_lin, L0_gnn_b_lin):
    import jax
    import jax.numpy as jnp

    def _L0_gnn_ref(x, edge_index, w_ih, w_hh, b_ih, b_hh, w_lin, b_lin):
        import jax, jax.numpy as jnp
        import numpy as np
        N = 6250
        DEG = 16
        DIM = 128
        H = 128

        def _lstm_last(seq, w_ih, w_hh, b):
            n = seq.shape[0]
            h_dim = w_hh.shape[1]
            h0 = jnp.zeros((n, h_dim), seq.dtype)

            def step(carry, x_t):
                h, c = carry
                gates = x_t @ w_ih.T + h @ w_hh.T + b
                i, f, g, o = jnp.split(gates, 4, axis=-1)
                c = jax.nn.sigmoid(f) * c + jax.nn.sigmoid(i) * jnp.tanh(g)
                h = jax.nn.sigmoid(o) * jnp.tanh(c)
                return ((h, c), None)
            (h, _), _ = jax.lax.scan(step, (h0, h0), jnp.swapaxes(seq, 0, 1))
            return h
        n, d = x.shape
        deg = edge_index.shape[1] // n
        col = edge_index[1]
        seq = x[col].reshape(n, deg, d)
        h_last = _lstm_last(seq, w_ih, w_hh, b_ih + b_hh)
        return h_last @ w_lin.T + b_lin
    edge_index = jnp.stack([src, dst])
    h = jnp.maximum(_layernorm(x, axis=-1), 0.0)
    x = x + _L0_gnn_ref(h, edge_index, L0_gnn_w_ih, L0_gnn_w_hh, L0_gnn_b_ih, L0_gnn_b_hh, L0_gnn_w_lin, L0_gnn_b_lin)
    return x

_drawn_inputs = setup_inputs


def setup_inputs(seed=0):
    import zlib

    import numpy as np

    out = dict(_drawn_inputs(seed))
    spreads = {}
    factors = {'L0_gnn_b_ih': 3.97, 'L0_gnn_b_hh': 4.097}
    for name, (base, spread) in spreads.items():
        noise = np.random.default_rng([zlib.crc32(name.encode()), seed]).standard_normal(out[name].shape)
        drawn = base * np.exp(spread * noise) if base else spread * noise
        out[name] = jnp.asarray(drawn.astype(out[name].dtype))
    for name, factor in factors.items():
        out[name] = (out[name] * factor).astype(out[name].dtype)
    return out
```

```python
from contextlib import ExitStack

import concourse.bass as bass
from concourse import mybir

F32 = mybir.dt.float32
F32R = mybir.dt.float32r
I32 = mybir.dt.int32
U32 = mybir.dt.uint32
ALU = mybir.AluOpType
ACT = mybir.ActivationFunctionType

P = 128
EPS = 1e-5
FORGET, INPUT, OUTPUT, CAND = range(4)


def lstm_gnn(nc, x, steps, w_ih_t, w_hh_t, b_ih, b_hh, w_lin_t, b_lin, out):
    n_nodes, dim = x.shape
    n_steps, _, n_tiles = steps.shape
    hid = w_hh_t.shape[0]
    gates = 4 * hid
    assert dim == P and hid == P and n_tiles == -(-n_nodes // P)
    full_tiles = n_nodes // P
    tail = n_nodes - full_tiles * P
    assert tail > 0 and full_tiles % 4 == 0 and n_steps % 2 == 0 and n_steps >= 6

    TPG = 4
    W = TPG * P
    BIG = full_tiles // TPG
    GROUPS = BIG + 1
    BODY = 2 * GROUPS
    PASSES = n_steps // 2
    SLOTS = 4
    assert BIG % SLOTS == 0

    table = nc.dram_tensor("gate_table", (n_nodes, gates), F32, kind="Internal").ap()

    with ExitStack() as ctx:
        def sb(name, shape, dt=F32):
            return ctx.enter_context(nc.sbuf_tensor(name, shape, dt))

        def sem(name):
            return ctx.enter_context(nc.semaphore(name))

        x_sb = sb("x_sb", [P, n_tiles, dim])
        ident = sb("ident", [P, P])
        w_ih_sb = sb("w_ih_sb", [P, gates])
        w_hh_sb = sb("w_hh_sb", [P, gates])
        w_hh_hi = sb("w_hh_hi", [P, gates], F32R)
        w_hh_lo = sb("w_hh_lo", [P, gates], F32R)
        w_lin_sb = sb("w_lin_sb", [P, dim])
        bias2 = sb("bias2", [2, gates])
        ones2 = sb("ones2", [2, P])
        b_lin_row = sb("b_lin_row", [1, dim])
        bias_all = sb("bias_all", [P, gates])
        b_lin_all = sb("b_lin_all", [P, dim])
        stats = sb("stats", [P, n_tiles, 6])
        moments = sb("moments", [P, n_tiles, 2])
        norm_tmp = sb("norm_tmp", [P, 4, n_tiles])
        normed = sb("normed", [P, 2, dim])
        feat = sb("feat", [P, 2, P])
        table_rows = sb("table_rows", [P, 4, gates])
        step_idx = sb("step_idx", [P, 2, n_tiles], I32)
        rows = sb("rows", [P, SLOTS, TPG, gates])
        tail_rows = sb("tail_rows", [P, 2, gates])
        cell = sb("cell", [P, GROUPS + 2, W])
        h_hi = sb("h_hi", [P, GROUPS, W], F32R)
        h_lo = sb("h_lo", [P, GROUPS, W], F32R)
        sig = sb("sig", [P, 2, 3, W])
        prod = sb("prod", [P, 2, 2, W])
        tanh_c = sb("tanh_c", [P, 2, W])
        h_full = sb("h_full", [P, 2, W])
        out_sb = sb("out_sb", [P, 4, TPG, dim])
        ps = ctx.enter_context(nc.psum_tensor("ps", [P, 8, 512], F32))

        x_loaded = [sem(f"x_loaded{k}") for k in range(5)]
        weights_loaded = sem("weights_loaded")
        biases_loaded = sem("biases_loaded")
        idx_loaded = [sem(f"idx_loaded{s}") for s in range(2)]
        ones_set = sem("ones_set")
        ident_set = sem("ident_set")
        bias_summed = sem("bias_summed")
        bias_copied = sem("bias_copied")
        stats_done = sem("stats_done")
        moments_done = sem("moments_done")
        norm_step = sem("norm_step")
        sqrt_done = sem("sqrt_done")
        w_split = sem("w_split")
        tile_normed = sem("tile_normed")
        tile_transposed = sem("tile_transposed")
        feat_ready = sem("feat_ready")
        table_summed = sem("table_summed")
        table_row_ready = sem("table_row_ready")
        table_stored = [sem(f"table_stored{k}") for k in range(4)]
        residual_ready = sem("residual_ready")
        rows_landed = [sem(f"rows_landed{k}") for k in range(SLOTS)]
        tail_landed = [sem(f"tail_landed{s}") for s in range(2)]
        rows_used = sem("rows_used")
        gathers_cleared = sem("gathers_cleared")
        cand_summed = sem("cand_summed")
        gates_summed = sem("gates_summed")
        gates_active = sem("gates_active")
        products_done = sem("products_done")
        cell_ready = sem("cell_ready")
        tanh_c_ready = sem("tanh_c_ready")
        h_computed = sem("h_computed")
        h_hi_ready = sem("h_hi_ready")
        h_lo_ready = sem("h_lo_ready")
        projected = sem("projected")
        out_ready = sem("out_ready")
        out_stored = [sem(f"out_stored{k}") for k in range(4)]

        def width(g):
            return W if g < BIG else tail

        def wait_from_one(eng, s, value):
            if not isinstance(value, int) or value > 0:
                eng.wait_ge(s, value)

        def passes(eng, body):
            body(0)
            with eng.Fori(1, PASSES - 1) as i:
                body(i)
            body(PASSES - 1)

        X_CHUNK = full_tiles // 4
        STAT_UNROLL = 6
        assert X_CHUNK % STAT_UNROLL == 0

        block = ctx.enter_context(nc.Block())

        @block.sync
        def _(sp):
            xv = x[0:full_tiles * P, :].rearrange("(n p) d -> p n d", p=P)
            for k in range(4):
                t0 = k * X_CHUNK
                sp.dma_start(x_sb[:, t0:t0 + X_CHUNK, :], xv[:, t0:t0 + X_CHUNK, :]).then_inc(x_loaded[k], 16)
            sp.dma_start(x_sb[0:tail, full_tiles, :], x[full_tiles * P:n_nodes, :]).then_inc(x_loaded[4], 16)

            def store_tile(t, k, n):
                sp.wait_ge(table_row_ready, t + 1)
                sp.dma_start(table[bass.ds(t * P, n), :], table_rows[0:n, k, :]).then_inc(table_stored[k], 16)

            with sp.Fori(0, full_tiles // 4) as c:
                for k in range(4):
                    store_tile(4 * c + k, k, P)
            store_tile(full_tiles, 0, tail)

            def load_steps(i):
                for s in range(2):
                    wait_from_one(sp, rows_used, BODY * i + GROUPS * (s - 1))
                    t = 2 * i + s
                    sp.dma_start(step_idx[:, s, :], steps[bass.ds(t, 1), :, :].rearrange("a p n -> p (a n)")
                                 ).then_inc(idx_loaded[s], 16)

            passes(sp, load_steps)

            for g in range(GROUPS):
                sp.wait_ge(out_ready, g + 1)
                n0 = g * W
                if g < BIG:
                    sp.dma_start(out[n0:n0 + W, :].rearrange("(n p) d -> p n d", p=P), out_sb[:, g % 4, :, :]
                                 ).then_inc(out_stored[g % 4], 16)
                else:
                    sp.dma_start(out[n0:n_nodes, :], out_sb[0:tail, g % 4, 0, :]).then_inc(out_stored[g % 4], 16)
            for k in range(4):
                sp.wait_ge(out_stored[k], 16 * len(range(k, GROUPS, 4)))

        @block.gpsimd
        def _(pool):
            pool.memset(ident[:, :], 0.0).then_inc(ident_set, 1)
            pool.wait_ge(ident_set, 1)
            pool.affine_select(out=ident[:, :], in_=ident[:, :], compare_op=ALU.not_equal, fill=1.0,
                               base=0, pattern=[[-1, P]], channel_multiplier=1).then_inc(ident_set, 1)
            for k in range(4):
                pool.wait_ge(table_stored[k], 16 * len(range(k, n_tiles, 4)))

            def gather(i):
                for s in range(2):
                    t = 2 * i + s
                    pool.wait_ge(idx_loaded[s], 16 * (i + 1))
                    pool.sem_inc(gathers_cleared, 1)
                    for g in range(GROUPS):
                        unit = BODY * i + GROUPS * s + g
                        if g < BIG:
                            wait_from_one(pool, rows_used, unit - SLOTS + 1 if g >= SLOTS else unit - SLOTS)
                            pool.sem_inc(gathers_cleared, 1)
                            for j in range(TPG):
                                pool.indirect_dma_start(
                                    rows[:, g % SLOTS, j, :], None, table,
                                    bass.IndirectOffsetOnAxis(
                                        ap=step_idx[:, s, g * TPG + j:g * TPG + j + 1].bitcast(U32), axis=0),
                                ).then_inc(rows_landed[g % SLOTS], 16)
                        else:
                            wait_from_one(pool, rows_used, unit - BODY + 1)
                            pool.sem_inc(gathers_cleared, 1)
                            pool.indirect_dma_start(
                                tail_rows[0:tail, s, :], None, table,
                                bass.IndirectOffsetOnAxis(
                                    ap=step_idx[0:tail, s, full_tiles:full_tiles + 1].bitcast(U32), axis=0),
                            ).then_inc(tail_landed[s], 16)

            passes(pool, gather)

        @block.tensor
        def _(pe):
            pe.wait_ge(ones_set, 1)
            pe.wait_ge(biases_loaded, 48)
            nc.tensor.matmul(ps[:, 0, :], ones2[:, :], bias2[:, :], start=True, stop=True)
            nc.tensor.matmul(ps[:, 1, 0:dim], ones2[0:1, :], b_lin_row[:, :], start=True, stop=True
                             ).then_inc(bias_summed, 1)

            def table_tile(t, k, n):
                pe.wait_ge(tile_normed, t + 1)
                wait_from_one(pe, feat_ready, t - 1)
                nc.tensor.transpose(ps[:, 2 + k, 0:n], normed[0:n, k, :], ident[0:n, 0:n]
                                    ).then_inc(tile_transposed, 1)
                pe.wait_ge(feat_ready, t + 1)
                wait_from_one(pe, table_row_ready, t - 1)
                nc.tensor.matmul(ps[0:n, 4 + k, :], feat[:, k, 0:n], w_ih_sb[:, :], start=True, stop=True
                                 ).then_inc(table_summed, 1)

            pe.wait_ge(ident_set, 2)
            pe.wait_ge(weights_loaded, 48)
            for k in range(2):
                table_tile(k, k, P)
            with pe.Fori(1, full_tiles // 2) as c:
                for k in range(2):
                    table_tile(2 * c + k, k, P)
            table_tile(full_tiles, 0, tail)

            def gate_sums(i):
                for s in range(2):
                    for g in range(GROUPS):
                        unit = BODY * i + GROUPS * s + g
                        first_step = isinstance(i, int) and i == 0 and s == 0
                        base = 4 * ((GROUPS * s + g) % 2)
                        n = width(g)
                        wait_from_one(pe, gates_active, unit - 1)
                        if isinstance(unit, int) and unit < 2:
                            pe.wait_ge(table_row_ready, n_tiles)
                            pe.wait_ge(bias_copied, 1)
                        if g < BIG:
                            uses = (BIG // SLOTS) * (2 * i + s) + g // SLOTS + 1
                            pe.wait_ge(rows_landed[g % SLOTS], 16 * TPG * uses)
                        else:
                            pe.wait_ge(tail_landed[s], 16 * (i + 1))
                        for q in (CAND, FORGET, INPUT, OUTPUT):
                            for j in range(TPG if g < BIG else 1):
                                if g < BIG:
                                    src, m = rows[:, g % SLOTS, j, q * hid:(q + 1) * hid], P
                                else:
                                    src, m = tail_rows[0:tail, s, q * hid:(q + 1) * hid], tail
                                last = nc.tensor.matmul(ps[:, base + q, j * P:j * P + m], src, ident[0:m, 0:m],
                                                        start=(j == 0), stop=first_step, is_transpose=True,
                                                        skip_group_check=True)
                            if first_step and q == CAND:
                                last.then_inc(cand_summed, 1)
                        if first_step:
                            last.then_inc(rows_used, 1)
                            continue
                        last.then_inc(rows_used, 1)
                        pe.wait_ge(h_lo_ready, unit - GROUPS + 1)
                        for q in (CAND, FORGET, INPUT, OUTPUT):
                            acc = ps[:, base + q, 0:n]
                            hi = w_hh_hi[:, q * hid:(q + 1) * hid]
                            lo = w_hh_lo[:, q * hid:(q + 1) * hid]
                            nc.tensor.matmul(acc, hi, h_hi[:, g, 0:n], start=False, stop=False, skip_group_check=True)
                            nc.tensor.matmul(acc, hi, h_lo[:, g, 0:n], start=False, stop=False, skip_group_check=True)
                            last = nc.tensor.matmul(acc, lo, h_hi[:, g, 0:n], start=False, stop=True,
                                                    skip_group_check=True)
                            if q == CAND:
                                last.then_inc(cand_summed, 1)
                        last.then_inc(gates_summed, 1)

            pe.wait_ge(w_split, 2)
            passes(pe, gate_sums)

            pe.wait_ge(gates_active, n_steps * GROUPS)
            for g in range(GROUPS):
                pe.wait_ge(h_computed, (n_steps - 1) * GROUPS + g + 1)
                wait_from_one(pe, out_ready, g - 7)
                for j in range(TPG if g < BIG else 1):
                    m = P if g < BIG else tail
                    last = nc.tensor.matmul(ps[0:m, g % 8, j * dim:(j + 1) * dim], cell[:, g, j * P:j * P + m],
                                            w_lin_sb[:, :], start=(j == 0), stop=True, skip_group_check=True)
                last.then_inc(projected, 1)

        @block.scalar
        def _(act):
            act.dma_start(w_ih_sb[:, :], w_ih_t).then_inc(weights_loaded, 16)
            act.dma_start(bias2[0:1, :], b_ih.rearrange("(a n) -> a n", a=1)).then_inc(biases_loaded, 16)
            act.dma_start(bias2[1:2, :], b_hh.rearrange("(a n) -> a n", a=1)).then_inc(biases_loaded, 16)
            act.dma_start(b_lin_row[:, :], b_lin.rearrange("(a n) -> a n", a=1)).then_inc(biases_loaded, 16)
            act.dma_start(w_hh_sb[:, :], w_hh_t).then_inc(weights_loaded, 16)
            act.dma_start(w_lin_sb[:, :], w_lin_t).then_inc(weights_loaded, 16)

            act.wait_ge(norm_step, 1)
            nc.scalar.activation(norm_tmp[:, 1, :], norm_tmp[:, 0, :], ACT.Sqrt).then_inc(sqrt_done, 1)

            def relu_tile(t, k, n):
                act.wait_ge(tile_transposed, t + 1)
                wait_from_one(act, table_summed, t - 1)
                nc.scalar.activation(feat[:, k, 0:n], ps[:, 2 + k, 0:n], ACT.Relu).then_inc(feat_ready, 1)

            for k in range(2):
                relu_tile(k, k, P)
            with act.Fori(1, full_tiles // 2) as c:
                for k in range(2):
                    relu_tile(2 * c + k, k, P)
            relu_tile(full_tiles, 0, tail)

            def activate_gates(unit, k, first_step):
                g, b, n = k % GROUPS, k % 2, width(k % GROUPS)
                base = 4 * b
                act.wait_ge(cand_summed, unit + 1)
                wait_from_one(act, products_done, unit - 1)
                nc.scalar.activation(cell[:, GROUPS + b, 0:n], ps[:, base + CAND, 0:n], ACT.Tanh)
                act.wait_ge(rows_used if first_step else gates_summed, unit + 1 if first_step else unit + 1 - GROUPS)
                wait_from_one(act, h_computed, unit - 1)
                nc.scalar.activation(sig[:, b, :, 0:n], ps[:, base:base + 3, 0:n], ACT.Sigmoid
                                     ).then_inc(gates_active, 1)

            def tanh_cell(unit, k, first_step):
                g, n = k % GROUPS, width(k % GROUPS)
                if first_step:
                    act.wait_ge(products_done, unit + 1)
                else:
                    act.wait_ge(cell_ready, unit + 1 - GROUPS)
                nc.scalar.activation(tanh_c[:, k % 2, 0:n], cell[:, g, 0:n], ACT.Tanh).then_inc(tanh_c_ready, 1)

            def round_h(unit, k):
                g, n = k % GROUPS, width(k % GROUPS)
                act.wait_ge(h_computed, unit + 1)
                nc.scalar.activation(h_hi[:, g, 0:n], h_full[:, k % 2, 0:n], ACT.Copy).then_inc(h_hi_ready, 1)

            def activations(i):
                first = isinstance(i, int) and i == 0
                last = isinstance(i, int) and i == PASSES - 1
                if first:
                    activate_gates(0, 0, True)
                for k in range(BODY):
                    unit = BODY * i + k
                    if not (last and k == BODY - 1):
                        activate_gates(unit + 1, (k + 1) % BODY, first and k + 1 < GROUPS)
                    tanh_cell(unit, k, first and k < GROUPS)
                    if not (first and k == 0) and not (last and k > GROUPS):
                        round_h(unit - 1, (k - 1) % BODY)

            passes(act, activations)

        @block.vector
        def _(dve):
            nc.vector.memset(ones2[:, :], 1.0).then_inc(ones_set, 1)
            nc.vector.memset(moments[:, :, :], 1.0).then_inc(moments_done, 1)
            dve.wait_ge(moments_done, 1)

            def row_stats(t, n):
                nc.vector.bn_stats(stats[0:n, t, :], x_sb[0:n, t, :]).then_inc(stats_done, 1)

            def row_moments(t, n):
                dve.wait_ge(stats_done, t + 1)
                nc.vector.bn_aggr(moments[0:n, t, :], stats[0:n, t, :]).then_inc(moments_done, 1)

            for c in range(4):
                dve.wait_ge(x_loaded[c], 16)
                with dve.Fori(c * X_CHUNK // STAT_UNROLL, (c + 1) * X_CHUNK // STAT_UNROLL) as r:
                    for k in range(STAT_UNROLL):
                        t = STAT_UNROLL * r + k
                        nc.vector.bn_stats(stats[:, bass.ds(t, 1), :].rearrange("p a s -> p (a s)"),
                                           x_sb[:, bass.ds(t, 1), :].rearrange("p a d -> p (a d)")
                                           ).then_inc(stats_done, 1)
            dve.wait_ge(x_loaded[4], 16)
            row_stats(full_tiles, tail)
            for t in range(n_tiles):
                row_moments(t, P if t < full_tiles else tail)

            dve.wait_ge(moments_done, n_tiles + 1)
            var_eps, root, inv, tmp = (norm_tmp[:, k, :] for k in range(4))
            nc.vector.tensor_scalar(var_eps, moments[:, :, 1], EPS, None, ALU.add).then_inc(norm_step, 1)
            dve.wait_ge(sqrt_done, 1)
            nc.vector.reciprocal(inv, root).then_inc(norm_step, 1)
            dve.wait_ge(norm_step, 2)
            nc.vector.tensor_tensor(tmp, inv, inv, ALU.mult).then_inc(norm_step, 1)
            dve.wait_ge(norm_step, 3)
            nc.vector.tensor_tensor(root, tmp, var_eps, ALU.mult).then_inc(norm_step, 1)
            dve.wait_ge(norm_step, 4)
            nc.vector.tensor_scalar(tmp, root, -0.5, 1.5, ALU.mult, ALU.add).then_inc(norm_step, 1)
            dve.wait_ge(norm_step, 5)
            nc.vector.tensor_tensor(root, inv, tmp, ALU.mult).then_inc(norm_step, 1)
            dve.wait_ge(bias_summed, 1)
            nc.vector.tensor_copy(bias_all[:, :], ps[:, 0, :])
            nc.vector.tensor_copy(b_lin_all[:, :], ps[:, 1, 0:dim]).then_inc(bias_copied, 1)
            dve.wait_ge(norm_step, 6)
            dve.wait_ge(bias_copied, 1)

            def norm_tile(t, k, n):
                wait_from_one(dve, tile_transposed, t - 1)
                nc.vector.tensor_scalar(normed[0:n, k, :], x_sb[0:n, bass.ds(t, 1), :].rearrange("p a d -> p (a d)"),
                                        moments[0:n, bass.ds(t, 1), 0:1].rearrange("p a s -> p (a s)"),
                                        norm_tmp[0:n, 1, bass.ds(t, 1)],
                                        ALU.subtract, ALU.mult).then_inc(tile_normed, 1)

            def bias_tile(t, b, k, n):
                dve.wait_ge(table_summed, t + 1)
                wait_from_one(dve, table_stored[k], 4 * (t - k))
                nc.vector.tensor_tensor(table_rows[0:n, k, :], ps[0:n, 4 + b, :], bias_all[0:n, :], ALU.add
                                        ).then_inc(table_row_ready, 1)

            norm_tile(0, 0, P)
            for k in range(4):
                norm_tile(k + 1, (k + 1) % 2, P)
                bias_tile(k, k % 2, k, P)
            with dve.Fori(1, full_tiles // 4 - 1) as c:
                for k in range(4):
                    norm_tile(4 * c + k + 1, (k + 1) % 2, P)
                    bias_tile(4 * c + k, k % 2, k, P)
            for k in range(4):
                t = full_tiles - 4 + k
                norm_tile(t + 1, (k + 1) % 2, P if t + 1 < full_tiles else tail)
                bias_tile(t, k % 2, k, P)
            bias_tile(full_tiles, 0, 0, tail)

            dve.wait_ge(weights_loaded, 48)
            nc.vector.tensor_copy(w_hh_hi[:, :], w_hh_sb[:, :]).then_inc(w_split, 1)
            dve.wait_ge(w_split, 1)
            nc.vector.tensor_tensor(w_hh_lo[:, :], w_hh_sb[:, :], w_hh_hi[:, :].bitcast(F32), ALU.subtract
                                    ).then_inc(w_split, 1)
            blin = b_lin_all[:, :].rearrange("p (a d) -> p a d", a=1)
            nc.vector.tensor_tensor(x_sb[:, 0:full_tiles, :], x_sb[:, 0:full_tiles, :],
                                    blin.to_broadcast([P, full_tiles, dim]), ALU.add)
            nc.vector.tensor_tensor(x_sb[0:tail, full_tiles, :], x_sb[0:tail, full_tiles, :], b_lin_all[0:tail, :],
                                    ALU.add).then_inc(residual_ready, 1)

            def products(unit, k, first_step):
                g, b, n = k % GROUPS, k % 2, width(k % GROUPS)
                dve.wait_ge(gates_active, unit + 1)
                if first_step:
                    nc.vector.tensor_tensor(cell[:, g, 0:n], sig[:, b, INPUT, 0:n], cell[:, GROUPS + b, 0:n],
                                            ALU.mult).then_inc(products_done, 1)
                else:
                    wait_from_one(dve, cell_ready, unit - 1 - GROUPS)
                    pair = cell[:, g:GROUPS + b + 1:GROUPS + b - g, 0:n]
                    nc.vector.tensor_tensor(prod[:, b, :, 0:n], sig[:, b, FORGET:INPUT + 1, 0:n], pair, ALU.mult
                                            ).then_inc(products_done, 1)

            def new_cell(unit, k):
                g, b, n = k % GROUPS, k % 2, width(k % GROUPS)
                dve.wait_ge(products_done, unit + 1)
                nc.vector.tensor_tensor(cell[:, g, 0:n], prod[:, b, 0, 0:n], prod[:, b, 1, 0:n], ALU.add
                                        ).then_inc(cell_ready, 1)

            def new_h(unit, k, last_step):
                g, b, n = k % GROUPS, k % 2, width(k % GROUPS)
                dve.wait_ge(tanh_c_ready, unit + 1)
                if not last_step:
                    wait_from_one(dve, h_lo_ready, unit - 1)
                dst = cell[:, g, 0:n] if last_step else h_full[:, b, 0:n]
                nc.vector.tensor_tensor(dst, sig[:, b, OUTPUT, 0:n], tanh_c[:, b, 0:n], ALU.mult
                                        ).then_inc(h_computed, 1)

            def low_h(unit, k):
                g, b, n = k % GROUPS, k % 2, width(k % GROUPS)
                dve.wait_ge(h_hi_ready, unit + 1)
                nc.vector.tensor_tensor(h_lo[:, g, 0:n], h_full[:, b, 0:n], h_hi[:, g, 0:n].bitcast(F32),
                                        ALU.subtract).then_inc(h_lo_ready, 1)

            def updates(i):
                first = isinstance(i, int) and i == 0
                last = isinstance(i, int) and i == PASSES - 1
                if first:
                    products(0, 0, True)
                for k in range(BODY):
                    unit = BODY * i + k
                    more = not (last and k == BODY - 1)
                    next_first = first and k + 1 < GROUPS
                    if more:
                        products(unit + 1, (k + 1) % BODY, next_first)
                    new_h(unit, k, last and k >= GROUPS)
                    if more and not next_first:
                        new_cell(unit + 1, (k + 1) % BODY)
                    if not (first and k == 0) and not (last and k > GROUPS):
                        low_h(unit - 1, (k - 1) % BODY)

            passes(dve, updates)

            dve.wait_ge(residual_ready, 1)
            for g in range(GROUPS):
                dve.wait_ge(projected, g + 1)
                wait_from_one(dve, out_stored[g % 4], 16 * (g // 4))
                tiles = slice(g * TPG, g * TPG + TPG) if g < BIG else slice(full_tiles, n_tiles)
                m, c = (P, TPG) if g < BIG else (tail, 1)
                nc.vector.tensor_tensor(out_sb[0:m, g % 4, 0:c, :],
                                        ps[0:m, g % 8, 0:c * dim].rearrange("p (a d) -> p a d", a=c),
                                        x_sb[0:m, tiles, :], ALU.add).then_inc(out_ready, 1)


_OUT = ((6250, 128), "float32")


def kernel(x, src, dst, L0_gnn_w_ih, L0_gnn_w_hh, L0_gnn_b_ih, L0_gnn_b_hh, L0_gnn_w_lin, L0_gnn_b_lin):
    import numpy as np
    import concourse.bacc as bacc
    from concourse.bass_utils import run_bass_kernel_spmd

    x = np.ascontiguousarray(x)
    n, dim = x.shape
    tiles = -(-n // P)
    dst = np.asarray(dst).reshape(n, -1)
    padded = np.zeros((tiles * P, dst.shape[1]), dst.dtype)
    padded[:n] = dst
    steps = np.ascontiguousarray(padded.reshape(tiles, P, -1).transpose(2, 1, 0))

    def reorder(a):
        i, f, g, o = np.split(np.asarray(a), 4, axis=0)
        return np.concatenate([f, i, o, g], axis=0)

    arrays = {
        "x": x,
        "steps": steps,
        "w_ih_t": np.ascontiguousarray(reorder(L0_gnn_w_ih).T),
        "w_hh_t": np.ascontiguousarray(reorder(L0_gnn_w_hh).T),
        "b_ih": reorder(L0_gnn_b_ih),
        "b_hh": reorder(L0_gnn_b_hh),
        "w_lin_t": np.ascontiguousarray(np.asarray(L0_gnn_w_lin).T),
        "b_lin": np.ascontiguousarray(L0_gnn_b_lin),
    }
    nc = bacc.Bacc("TRN2", target_bir_lowering=False, num_devices=1)
    args = [nc.dram_tensor(k, a.shape, mybir.dt.from_np(a.dtype), kind="ExternalInput").ap()
            for k, a in arrays.items()]
    out = nc.dram_tensor("out", _OUT[0], mybir.dt.from_np(np.dtype(_OUT[1])), kind="ExternalOutput").ap()
    lstm_gnn(nc, *args, out)
    r = run_bass_kernel_spmd(nc, [arrays], core_ids=[0])
    return r.results[0]["out"]
```

```python
from contextlib import ExitStack

import concourse.bass as bass
from concourse import mybir

F32 = mybir.dt.float32
F32R = mybir.dt.float32r
I32 = mybir.dt.int32
U32 = mybir.dt.uint32
ALU = mybir.AluOpType
ACT = mybir.ActivationFunctionType

P = 128
EPS = 1e-5
FORGET, INPUT, OUTPUT, CAND = range(4)


class Batch:

    def __init__(self, groups, tail_group, n_steps, before):
        self.groups, self.tail_group, self.before = groups, tail_group, before
        self.width = len(groups)
        self.full_width = sum(g != tail_group for g in groups)
        self.body = 2 * self.width
        self.passes = n_steps // 2
        past = [(b.width, b.full_width) for b in before]
        self.unit0 = n_steps * sum(w for w, _ in past)
        self.full0 = n_steps * sum(f for _, f in past)
        self.recurrent0 = (n_steps - 1) * sum(w for w, _ in past)
        self.split0 = (n_steps - 1) * sum(f for _, f in past)

    def group(self, k):
        return self.groups[k % self.width]

    def is_tail(self, k):
        return self.group(k) == self.tail_group

    def first_step(self, i, k):
        return isinstance(i, int) and i == 0 and k < self.width

    def last_step(self, i, k):
        return isinstance(i, int) and i == self.passes - 1 and k >= self.width

    def _full(self, k):
        return self.full_width * (k // self.width) + sum(g != self.tail_group for g in self.groups[:k % self.width])

    def units(self, i, k):
        return self.unit0 + self.body * i + k

    def fulls(self, i, k):
        return self.full0 + 2 * self.full_width * i + self._full(k)

    def recurrents(self, i, k):
        return self.recurrent0 + self.body * i + k - self.width

    def splits(self, i, k):
        return self.split0 + 2 * self.full_width * i + self._full(k)


def lstm_gnn(nc, x, steps, w_ih_t, w_hh_t, b_ih, b_hh, w_lin_t, b_lin, out):
    n_nodes, dim = x.shape
    n_steps, _, n_tiles = steps.shape
    hid = w_hh_t.shape[0]
    gates = 4 * hid
    assert dim == P and hid == P and n_tiles == -(-n_nodes // P)
    full_tiles = n_nodes // P
    tail = n_nodes - full_tiles * P
    assert tail > 0 and full_tiles % 4 == 0 and n_steps % 2 == 0 and n_steps >= 6

    TPG = 4
    W = TPG * P
    BIG = full_tiles // TPG
    GROUPS = BIG + 1
    SLOTS = 6
    half = BIG // 2
    first_half = Batch(list(range(half)), BIG, n_steps, [])
    mid = half + half // 2
    second_half = Batch([*range(half, mid), BIG, *range(mid, BIG)], BIG, n_steps, [first_half])
    batches = [first_half, second_half]
    for b in batches:
        assert 2 * b.full_width % SLOTS == 0 and b.full0 % SLOTS == 0 and b.unit0 % 2 == 0
        assert not b.is_tail(0) and not b.is_tail(b.body - 1)
    n_units = n_steps * GROUPS

    table = nc.dram_tensor("gate_table", (n_nodes, gates), F32, kind="Internal").ap()

    with ExitStack() as ctx:
        def sb(name, shape, dt=F32):
            return ctx.enter_context(nc.sbuf_tensor(name, shape, dt))

        def sem(name):
            return ctx.enter_context(nc.semaphore(name))

        x_sb = sb("x_sb", [P, n_tiles, dim])
        ident = sb("ident", [P, P])
        w_ih_sb = sb("w_ih_sb", [P, gates])
        w_hh_sb = sb("w_hh_sb", [P, gates])
        w_hh_hi = sb("w_hh_hi", [P, gates], F32R)
        w_hh_lo = sb("w_hh_lo", [P, gates], F32R)
        w_lin_sb = sb("w_lin_sb", [P, dim])
        bias2 = sb("bias2", [2, gates])
        ones2 = sb("ones2", [2, P])
        b_lin_row = sb("b_lin_row", [1, dim])
        bias_all = sb("bias_all", [P, gates])
        b_lin_all = sb("b_lin_all", [P, dim])
        stats = sb("stats", [P, n_tiles, 6])
        moments = sb("moments", [P, n_tiles, 2])
        var_eps, root, inv_root, newton, scale, shift = (
            sb(name, [P, n_tiles]) for name in ("var_eps", "root", "inv_root", "newton", "scale", "shift"))
        normed = sb("normed", [P, 2, dim])
        feat = sb("feat", [P, 2, P])
        step_idx = sb("step_idx", [P, 2, n_tiles], I32)
        rows = sb("rows", [P, SLOTS, TPG, gates])
        table_rows = rows[:, 0, :, :]
        out_sb = rows[:, 1, :, :].rearrange("p b (a d) -> p b a d", d=dim)
        tail_rows = sb("tail_rows", [P, 2, gates])
        cell = sb("cell", [P, GROUPS + 2, W])
        h_hi = sb("h_hi", [P, BIG, W], F32R)
        h_lo = sb("h_lo", [P, BIG, W], F32R)
        sig = sb("sig", [P, 2, 3, W])
        prod = sb("prod", [P, 2, 2, W])
        tanh_c = sb("tanh_c", [P, 2, W])
        h_full = sb("h_full", [P, 2, W])
        h_tail = sb("h_tail", [P, tail])
        ps = ctx.enter_context(nc.psum_tensor("ps", [P, 8, 512], F32))

        x_loaded = [sem(f"x_loaded{k}") for k in range(5)]
        weights_loaded = sem("weights_loaded")
        biases_loaded = sem("biases_loaded")
        idx_loaded = [sem(f"idx_loaded{s}") for s in range(2)]
        ones_set = sem("ones_set")
        ident_set = sem("ident_set")
        bias_summed = sem("bias_summed")
        bias_copied = sem("bias_copied")
        stats_done = sem("stats_done")
        moments_done = sem("moments_done")
        root_step = sem("root_step")
        sqrt_done = sem("sqrt_done")
        scales_ready = sem("scales_ready")
        w_split = sem("w_split")
        tile_normed = sem("tile_normed")
        tile_transposed = sem("tile_transposed")
        feat_ready = sem("feat_ready")
        table_summed = sem("table_summed")
        table_row_ready = sem("table_row_ready")
        table_stored = [sem(f"table_stored{k}") for k in range(4)]
        residual_ready = sem("residual_ready")
        rows_landed = [sem(f"rows_landed{k}") for k in range(SLOTS)]
        tail_landed = [sem(f"tail_landed{s}") for s in range(2)]
        rows_used = sem("rows_used")
        tail_used = sem("tail_used")
        gathers_cleared = sem("gathers_cleared")
        cand_summed = sem("cand_summed")
        gates_summed = sem("gates_summed")
        cand_active = sem("cand_active")
        gates_active = sem("gates_active")
        products_done = sem("products_done")
        cell_ready = sem("cell_ready")
        tanh_c_ready = sem("tanh_c_ready")
        h_computed = sem("h_computed")
        h_hi_ready = sem("h_hi_ready")
        h_lo_ready = sem("h_lo_ready")
        projected = sem("projected")
        out_ready = sem("out_ready")
        out_stored = [sem(f"out_stored{k}") for k in range(4)]

        def width(g):
            return W if g < BIG else tail

        def wait_from_one(eng, s, value):
            if not isinstance(value, int) or value > 0:
                eng.wait_ge(s, value)

        def passes(eng, body):
            for b in batches:
                body(b, 0)
                with eng.Fori(1, b.passes - 1) as i:
                    body(b, i)
                body(b, b.passes - 1)

        def next_unit(b, i, k):
            if k + 1 < b.body:
                return b, i, k + 1
            if not (isinstance(i, int) and i == b.passes - 1):
                return b, i + 1, 0
            return (batches[1], 0, 0) if b is batches[0] else None

        def split_before(b, i, k):
            if k == 0:
                return None if isinstance(i, int) and i == 0 else (b, i - 1, b.body - 1)
            return None if b.is_tail(k - 1) or b.last_step(i, k - 1) else (b, i, k - 1)

        CHUNKS = 4
        CHUNK = full_tiles // CHUNKS
        ROOT_OPS = 6
        assert CHUNK == 12 and CHUNK % 4 == 0

        block = ctx.enter_context(nc.Block())

        @block.sync
        def _(sp):
            xv = x[0:full_tiles * P, :].rearrange("(n p) d -> p n d", p=P)
            for c in range(CHUNKS):
                t0 = c * CHUNK
                sp.dma_start(x_sb[:, t0:t0 + CHUNK, :], xv[:, t0:t0 + CHUNK, :]).then_inc(x_loaded[c], 16)
                if c == 0:
                    sp.dma_start(x_sb[0:tail, full_tiles, :], x[full_tiles * P:n_nodes, :]
                                 ).then_inc(x_loaded[CHUNKS], 16)

            def store_tile(t, k, n):
                sp.wait_ge(table_row_ready, t + 1)
                sp.dma_start(table[bass.ds(t * P, n), :], table_rows[0:n, k, :]).then_inc(table_stored[k], 16)

            with sp.Fori(0, full_tiles // 4) as c:
                for k in range(4):
                    store_tile(4 * c + k, k, P)
            store_tile(full_tiles, 0, tail)

            def load_steps(b, i):
                for s in range(2):
                    wait_from_one(sp, rows_used, b.fulls(i, b.width * s) - b.full_width)
                    if b.tail_group in b.groups:
                        wait_from_one(sp, tail_used, 2 * i + s - 1)
                    t = 2 * i + s
                    sp.dma_start(step_idx[:, s, :], steps[bass.ds(t, 1), :, :].rearrange("a p n -> p (a n)")
                                 ).then_inc(idx_loaded[s], 16)

            passes(sp, load_steps)

            for g in range(GROUPS):
                sp.wait_ge(out_ready, g + 1)
                n0 = g * W
                if g < BIG:
                    sp.dma_start(out[n0:n0 + W, :].rearrange("(n p) d -> p n d", p=P), out_sb[:, g % 4, :, :]
                                 ).then_inc(out_stored[g % 4], 16)
                else:
                    sp.dma_start(out[n0:n_nodes, :], out_sb[0:tail, g % 4, 0, :]).then_inc(out_stored[g % 4], 16)
            for k in range(4):
                sp.wait_ge(out_stored[k], 16 * len(range(k, GROUPS, 4)))

        @block.gpsimd
        def _(pool):
            pool.memset(ident[:, :], 0.0).then_inc(ident_set, 1)
            pool.wait_ge(ident_set, 1)
            pool.affine_select(out=ident[:, :], in_=ident[:, :], compare_op=ALU.not_equal, fill=1.0,
                               base=0, pattern=[[-1, P]], channel_multiplier=1).then_inc(ident_set, 1)
            for k in range(4):
                pool.wait_ge(table_stored[k], 16 * len(range(k, n_tiles, 4)))

            def gather(b, i):
                for k in range(b.body):
                    g, s = b.group(k), k // b.width
                    if k % b.width == 0:
                        pool.wait_ge(idx_loaded[s], 16 * (b.passes * len(b.before) + i + 1))
                        pool.sem_inc(gathers_cleared, 1)
                    if b.is_tail(k):
                        wait_from_one(pool, tail_used, 2 * i + s - 1)
                        pool.sem_inc(gathers_cleared, 1)
                        pool.indirect_dma_start(
                            tail_rows[0:tail, s, :], None, table,
                            bass.IndirectOffsetOnAxis(
                                ap=step_idx[0:tail, s, full_tiles:full_tiles + 1].bitcast(U32), axis=0),
                        ).then_inc(tail_landed[s], 16)
                        continue
                    slot = b.fulls(0, k) % SLOTS
                    wait_from_one(pool, rows_used, b.fulls(i, k) - SLOTS + 1)
                    pool.sem_inc(gathers_cleared, 1)
                    for j in range(TPG):
                        pool.indirect_dma_start(
                            rows[:, slot, j, :], None, table,
                            bass.IndirectOffsetOnAxis(
                                ap=step_idx[:, s, g * TPG + j:g * TPG + j + 1].bitcast(U32), axis=0),
                        ).then_inc(rows_landed[slot], 16)

            passes(pool, gather)

        @block.tensor
        def _(pe):
            pe.wait_ge(ones_set, 1)
            pe.wait_ge(biases_loaded, 48)
            nc.tensor.matmul(ps[:, 0, :], ones2[:, :], bias2[:, :], start=True, stop=True)
            nc.tensor.matmul(ps[:, 1, 0:dim], ones2[0:1, :], b_lin_row[:, :], start=True, stop=True
                             ).then_inc(bias_summed, 1)

            def transpose_tile(t, b, n):
                pe.wait_ge(tile_normed, t + 1)
                wait_from_one(pe, feat_ready, t - 1)
                nc.tensor.transpose(ps[:, 2 + b, 0:n], normed[0:n, b, :], ident[0:n, 0:n]
                                    ).then_inc(tile_transposed, 1)

            def table_tile(t, k, n):
                pe.wait_ge(feat_ready, t + 1)
                wait_from_one(pe, table_row_ready, t - 3)
                nc.tensor.matmul(ps[0:n, 4 + k, :], feat[:, k % 2, 0:n], w_ih_sb[:, :], start=True, stop=True
                                 ).then_inc(table_summed, 1)

            def four_tiles(c):
                last = isinstance(c, int) and c == full_tiles // 4 - 1
                for k in range(4):
                    transpose_tile(4 * c + k + 1, (k + 1) % 2, tail if last and k == 3 else P)
                    table_tile(4 * c + k, k, P)

            pe.wait_ge(ident_set, 2)
            pe.wait_ge(weights_loaded, 48)
            transpose_tile(0, 0, P)
            four_tiles(0)
            with pe.Fori(1, full_tiles // 4 - 1) as c:
                four_tiles(c)
            four_tiles(full_tiles // 4 - 1)
            table_tile(full_tiles, 0, tail)

            def gate_sums(b, i):
                for k in range(b.body):
                    g, s = b.group(k), k // b.width
                    is_tail, first_step = b.is_tail(k), b.first_step(i, k)
                    base, n = 4 * (k % 2), width(g)
                    unit = b.units(i, k)
                    wait_from_one(pe, cand_active, unit - 1)
                    if isinstance(unit, int) and unit < 2:
                        pe.wait_ge(feat_ready, n_tiles)
                        pe.wait_ge(table_row_ready, n_tiles)
                        pe.wait_ge(bias_copied, 1)
                    slot = b.fulls(0, k) % SLOTS
                    if is_tail:
                        pe.wait_ge(tail_landed[s], 16 * (i + 1))
                        tiles = [(tail_rows[0:tail, s, :], tail)]
                    else:
                        uses = b.full0 // SLOTS + 2 * b.full_width // SLOTS * i + (b.fulls(0, k) - b.full0) // SLOTS + 1
                        pe.wait_ge(rows_landed[slot], 16 * TPG * uses)
                        tiles = [(rows[:, slot, j, :], P) for j in range(TPG)]
                    for q in (CAND, FORGET, INPUT, OUTPUT):
                        if q == FORGET:
                            wait_from_one(pe, gates_active, unit - 1)
                        for j, (src, m) in enumerate(tiles):
                            last = nc.tensor.matmul(ps[:, base + q, j * P:j * P + m], src[:, q * hid:(q + 1) * hid],
                                                    ident[0:m, 0:m], start=(j == 0), stop=first_step,
                                                    is_transpose=True, skip_group_check=True)
                        if first_step and q == CAND:
                            last.then_inc(cand_summed, 1)
                    last.then_inc(tail_used if is_tail else rows_used, 1)
                    if first_step:
                        continue
                    if is_tail:
                        pe.wait_ge(h_computed, unit - b.width + 1)
                        for q in (CAND, FORGET, INPUT, OUTPUT):
                            last = nc.tensor.matmul(ps[:, base + q, 0:n], w_hh_sb[:, q * hid:(q + 1) * hid],
                                                    h_tail[:, :], start=False, stop=True, skip_group_check=True)
                            if q == CAND:
                                last.then_inc(cand_summed, 1)
                        last.then_inc(gates_summed, 1)
                        continue
                    pe.wait_ge(h_lo_ready, b.splits(i, k) - b.full_width + 1)
                    for q in (CAND, FORGET, INPUT, OUTPUT):
                        acc = ps[:, base + q, 0:n]
                        hi = w_hh_hi[:, q * hid:(q + 1) * hid]
                        lo = w_hh_lo[:, q * hid:(q + 1) * hid]
                        nc.tensor.matmul(acc, hi, h_hi[:, g, 0:n], start=False, stop=False, skip_group_check=True)
                        nc.tensor.matmul(acc, hi, h_lo[:, g, 0:n], start=False, stop=False, skip_group_check=True)
                        last = nc.tensor.matmul(acc, lo, h_hi[:, g, 0:n], start=False, stop=True,
                                                skip_group_check=True)
                        if q == CAND:
                            last.then_inc(cand_summed, 1)
                    last.then_inc(gates_summed, 1)

            pe.wait_ge(w_split, 2)
            passes(pe, gate_sums)

            for g in range(GROUPS):
                pe.wait_ge(gates_active, n_units - 1 if g < 4 else n_units)
                b = first_half if g < half else second_half
                pe.wait_ge(h_computed, b.units(b.passes - 1, b.width + b.groups.index(g)) + 1)
                wait_from_one(pe, out_ready, g - 7)
                for j in range(TPG if g < BIG else 1):
                    m = P if g < BIG else tail
                    last = nc.tensor.matmul(ps[0:m, g % 8, j * dim:(j + 1) * dim], cell[:, g, j * P:j * P + m],
                                            w_lin_sb[:, :], start=(j == 0), stop=True, skip_group_check=True)
                last.then_inc(projected, 1)

        @block.scalar
        def _(act):
            act.dma_start(w_ih_sb[:, :], w_ih_t).then_inc(weights_loaded, 16)
            act.dma_start(bias2[0:1, :], b_ih.rearrange("(a n) -> a n", a=1)).then_inc(biases_loaded, 16)
            act.dma_start(bias2[1:2, :], b_hh.rearrange("(a n) -> a n", a=1)).then_inc(biases_loaded, 16)
            act.dma_start(b_lin_row[:, :], b_lin.rearrange("(a n) -> a n", a=1)).then_inc(biases_loaded, 16)
            act.dma_start(w_hh_sb[:, :], w_hh_t).then_inc(weights_loaded, 16)
            act.dma_start(w_lin_sb[:, :], w_lin_t).then_inc(weights_loaded, 16)

            def take_roots(chunk, cols):
                act.wait_ge(root_step, ROOT_OPS * chunk + 1)
                nc.scalar.activation(root[:, cols], var_eps[:, cols], ACT.Sqrt).then_inc(sqrt_done, 1)

            def norm_tile(t, b, n, chunk):
                act.wait_ge(scales_ready, chunk + 1)
                wait_from_one(act, tile_transposed, t - 1)
                col = 0 if n == tail else t + 1
                nc.scalar.activation(normed[0:n, b, :], x_sb[0:n, bass.ds(t, 1), :].rearrange("p a d -> p (a d)"),
                                     ACT.Identity, bias=shift[0:n, bass.ds(col, 1)],
                                     scale=scale[0:n, bass.ds(col, 1)]).then_inc(tile_normed, 1)

            def relu_tile(t, b, n):
                act.wait_ge(tile_transposed, t + 1)
                nc.scalar.activation(feat[:, b, 0:n], ps[:, 2 + b, 0:n], ACT.Relu).then_inc(feat_ready, 1)

            def feature_chunk(c):
                last = c == CHUNKS - 1
                for k in range(CHUNK):
                    t = CHUNK * c + k
                    relu_tile(t, k % 2, P)
                    if not (last and k == CHUNK - 1):
                        tail_next = last and k == CHUNK - 2
                        norm_tile(t + 2, k % 2, tail if tail_next else P,
                                  0 if tail_next else c + (k + 2) // CHUNK)
                    if c == 0 and k == 1:
                        take_roots(1, slice(CHUNK + 1, 2 * CHUNK + 1))
                    if c + 2 < CHUNKS and k == 8:
                        take_roots(c + 2, slice(CHUNK * (c + 2) + 1, CHUNK * (c + 3) + 1))

            take_roots(0, slice(0, CHUNK + 1))
            for k in range(2):
                norm_tile(k, k, P, 0)
            for c in range(CHUNKS):
                feature_chunk(c)
            relu_tile(full_tiles, 0, tail)

            def activate_gates(b, i, k):
                buf, n, unit = k % 2, width(b.group(k)), b.units(i, k)
                base = 4 * buf
                act.wait_ge(cand_summed, unit + 1)
                wait_from_one(act, products_done, unit - 1)
                nc.scalar.activation(cell[:, GROUPS + buf, 0:n], ps[:, base + CAND, 0:n], ACT.Tanh
                                     ).then_inc(cand_active, 1)
                if not b.first_step(i, k):
                    act.wait_ge(gates_summed, b.recurrents(i, k) + 1)
                elif b.is_tail(k):
                    act.wait_ge(tail_used, 1)
                else:
                    act.wait_ge(rows_used, b.fulls(i, k) + 1)
                wait_from_one(act, h_computed, unit - 1)
                nc.scalar.activation(sig[:, buf, :, 0:n], ps[:, base:base + 3, 0:n], ACT.Sigmoid
                                     ).then_inc(gates_active, 1)

            def tanh_cell(b, i, k):
                g, n = b.group(k), width(b.group(k))
                if b.first_step(i, k):
                    act.wait_ge(products_done, b.units(i, k) + 1)
                else:
                    act.wait_ge(cell_ready, b.recurrents(i, k) + 1)
                nc.scalar.activation(tanh_c[:, k % 2, 0:n], cell[:, g, 0:n], ACT.Tanh).then_inc(tanh_c_ready, 1)

            def round_h(b, i, k):
                act.wait_ge(h_computed, b.units(i, k) + 1)
                nc.scalar.activation(h_hi[:, b.group(k), :], h_full[:, b.fulls(0, k) % 2, :], ACT.Copy
                                     ).then_inc(h_hi_ready, 1)

            def activations(b, i):
                if isinstance(i, int) and i == 0 and not b.before:
                    activate_gates(b, 0, 0)
                for k in range(b.body):
                    if following := next_unit(b, i, k):
                        activate_gates(*following)
                    tanh_cell(b, i, k)
                    if split := split_before(b, i, k):
                        round_h(*split)

            passes(act, activations)

        @block.vector
        def _(dve):
            nc.vector.memset(ones2[:, :], 1.0).then_inc(ones_set, 1)
            nc.vector.memset(moments[:, :, :], 1.0).then_inc(moments_done, 1)
            dve.wait_ge(moments_done, 1)

            def row_stats(t, col, n):
                nc.vector.bn_stats(stats[0:n, bass.ds(col, 1), :].rearrange("p a s -> p (a s)"),
                                   x_sb[0:n, bass.ds(t, 1), :].rearrange("p a d -> p (a d)")
                                   ).then_inc(stats_done, 1)

            def row_moments(col, n, taken):
                dve.wait_ge(stats_done, taken)
                nc.vector.bn_aggr(moments[0:n, bass.ds(col, 1), :].rearrange("p a s -> p (a s)"),
                                  stats[0:n, bass.ds(col, 1), :].rearrange("p a s -> p (a s)")
                                  ).then_inc(moments_done, 1)

            def root_op(op, chunk, cols, taken):
                if op == 0:
                    dve.wait_ge(moments_done, taken)
                else:
                    dve.wait_ge(root_step, ROOT_OPS * chunk + op)
                if op == 0:
                    nc.vector.tensor_scalar(var_eps[:, cols], moments[:, cols, 1], EPS, None, ALU.add
                                            ).then_inc(root_step, 1)
                elif op == 1:
                    dve.wait_ge(sqrt_done, chunk + 1)
                    nc.vector.reciprocal(inv_root[:, cols], root[:, cols]).then_inc(root_step, 1)
                elif op == 2:
                    nc.vector.tensor_tensor(newton[:, cols], inv_root[:, cols], inv_root[:, cols], ALU.mult
                                            ).then_inc(root_step, 1)
                elif op == 3:
                    nc.vector.tensor_tensor(root[:, cols], newton[:, cols], var_eps[:, cols], ALU.mult
                                            ).then_inc(root_step, 1)
                elif op == 4:
                    nc.vector.tensor_scalar(newton[:, cols], root[:, cols], -0.5, 1.5, ALU.mult, ALU.add
                                            ).then_inc(root_step, 1)
                elif op == 5:
                    nc.vector.tensor_tensor(scale[:, cols], inv_root[:, cols], newton[:, cols], ALU.mult
                                            ).then_inc(root_step, 1)
                else:
                    nc.vector.scalar_tensor_tensor(out=shift[:, cols], in0=moments[:, cols, 0], scalar=-1.0,
                                                   in1=scale[:, cols], op0=ALU.mult, op1=ALU.mult
                                                   ).then_inc(scales_ready, 1)

            def bias_tile(t, k, n):
                dve.wait_ge(table_summed, t + 1)
                wait_from_one(dve, table_stored[k], 4 * (t - k))
                nc.vector.tensor_tensor(table_rows[0:n, k, :], ps[0:n, 4 + k, :], bias_all[0:n, :], ALU.add
                                        ).then_inc(table_row_ready, 1)

            dve.wait_ge(x_loaded[0], 16)
            for t in range(CHUNK):
                row_stats(t, t + 1, P)
            dve.wait_ge(x_loaded[CHUNKS], 16)
            row_stats(full_tiles, 0, tail)
            for col in range(1, CHUNK + 1):
                row_moments(col, P, col)
            row_moments(0, tail, CHUNK + 1)
            for op in range(ROOT_OPS + 1):
                root_op(op, 0, slice(0, CHUNK + 1), CHUNK + 2)
            dve.wait_ge(x_loaded[1], 16)
            for t in range(CHUNK, 2 * CHUNK):
                row_stats(t, t + 1, P)
            for col in range(CHUNK + 1, 2 * CHUNK + 1):
                row_moments(col, P, col + 1)
            for op in range(ROOT_OPS + 1):
                root_op(op, 1, slice(CHUNK + 1, 2 * CHUNK + 1), 2 * CHUNK + 2)
            dve.wait_ge(bias_summed, 1)
            nc.vector.tensor_copy(bias_all[:, :], ps[:, 0, :])
            nc.vector.tensor_copy(b_lin_all[:, :], ps[:, 1, 0:dim]).then_inc(bias_copied, 1)
            dve.wait_ge(bias_copied, 1)
            for c in range(2, CHUNKS):
                dve.wait_ge(x_loaded[c], 16)

            for c in range(CHUNKS - 2):
                cols = slice(CHUNK * (c + 2) + 1, CHUNK * (c + 3) + 1)
                for k in range(CHUNK):
                    pair = [CHUNK * (c + 2) + 2 * k + e for e in range(2)] if k < CHUNK // 2 else []
                    for t in pair:
                        row_stats(t, t + 1, P)
                    bias_tile(CHUNK * c + k, k % 4, P)
                    for t in pair:
                        row_moments(t + 1, P, t + 2)
                    for op in {6: (0,), 9: (1, 2), 10: (3, 4), 11: (5, 6)}.get(k, ()):
                        root_op(op, c + 2, cols, CHUNK * (c + 3) + 2)
            with dve.Fori(CHUNKS - 2, CHUNKS) as c:
                for k in range(CHUNK):
                    bias_tile(CHUNK * c + k, k % 4, P)
            bias_tile(full_tiles, 0, tail)

            dve.wait_ge(weights_loaded, 48)
            nc.vector.tensor_copy(w_hh_hi[:, :], w_hh_sb[:, :]).then_inc(w_split, 1)
            dve.wait_ge(w_split, 1)
            nc.vector.tensor_tensor(w_hh_lo[:, :], w_hh_sb[:, :], w_hh_hi[:, :].bitcast(F32), ALU.subtract
                                    ).then_inc(w_split, 1)
            blin = b_lin_all[:, :].rearrange("p (a d) -> p a d", a=1)
            nc.vector.tensor_tensor(x_sb[:, 0:full_tiles, :], x_sb[:, 0:full_tiles, :],
                                    blin.to_broadcast([P, full_tiles, dim]), ALU.add)
            nc.vector.tensor_tensor(x_sb[0:tail, full_tiles, :], x_sb[0:tail, full_tiles, :], b_lin_all[0:tail, :],
                                    ALU.add).then_inc(residual_ready, 1)

            def products(b, i, k):
                g, buf, n = b.group(k), k % 2, width(b.group(k))
                dve.wait_ge(gates_active, b.units(i, k) + 1)
                if b.first_step(i, k):
                    nc.vector.tensor_tensor(cell[:, g, 0:n], sig[:, buf, INPUT, 0:n], cell[:, GROUPS + buf, 0:n],
                                            ALU.mult).then_inc(products_done, 1)
                else:
                    after_first = isinstance(i, int) and i == 0 and k == b.width
                    wait_from_one(dve, cell_ready, b.recurrents(i, k) - (0 if after_first else 1))
                    pair = cell[:, g:GROUPS + buf + 1:GROUPS + buf - g, 0:n]
                    nc.vector.tensor_tensor(prod[:, buf, :, 0:n], sig[:, buf, FORGET:INPUT + 1, 0:n], pair, ALU.mult
                                            ).then_inc(products_done, 1)

            def new_cell(b, i, k):
                g, buf, n = b.group(k), k % 2, width(b.group(k))
                dve.wait_ge(products_done, b.units(i, k) + 1)
                nc.vector.tensor_tensor(cell[:, g, 0:n], prod[:, buf, 0, 0:n], prod[:, buf, 1, 0:n], ALU.add
                                        ).then_inc(cell_ready, 1)

            def new_h(b, i, k):
                g, buf, n = b.group(k), k % 2, width(b.group(k))
                dve.wait_ge(tanh_c_ready, b.units(i, k) + 1)
                if b.last_step(i, k):
                    dst = cell[:, g, 0:n]
                elif b.is_tail(k):
                    dst = h_tail[:, :]
                else:
                    wait_from_one(dve, h_lo_ready, b.splits(i, k) - 1)
                    dst = h_full[:, b.fulls(0, k) % 2, :]
                nc.vector.tensor_tensor(dst, sig[:, buf, OUTPUT, 0:n], tanh_c[:, buf, 0:n], ALU.mult
                                        ).then_inc(h_computed, 1)

            def low_h(b, i, k):
                g = b.group(k)
                dve.wait_ge(h_hi_ready, b.splits(i, k) + 1)
                nc.vector.tensor_tensor(h_lo[:, g, :], h_full[:, b.fulls(0, k) % 2, :], h_hi[:, g, :].bitcast(F32),
                                        ALU.subtract).then_inc(h_lo_ready, 1)

            def updates(b, i):
                if isinstance(i, int) and i == 0 and not b.before:
                    products(b, 0, 0)
                for k in range(b.body):
                    following = next_unit(b, i, k)
                    if following:
                        products(*following)
                    new_h(b, i, k)
                    if following and not following[0].first_step(*following[1:]):
                        new_cell(*following)
                    if split := split_before(b, i, k):
                        low_h(*split)

            passes(dve, updates)

            dve.wait_ge(residual_ready, 1)
            for g in range(GROUPS):
                dve.wait_ge(projected, g + 1)
                wait_from_one(dve, out_stored[g % 4], 16 * (g // 4))
                tiles = slice(g * TPG, g * TPG + TPG) if g < BIG else slice(full_tiles, n_tiles)
                m, c = (P, TPG) if g < BIG else (tail, 1)
                nc.vector.tensor_tensor(out_sb[0:m, g % 4, 0:c, :],
                                        ps[0:m, g % 8, 0:c * dim].rearrange("p (a d) -> p a d", a=c),
                                        x_sb[0:m, tiles, :], ALU.add).then_inc(out_ready, 1)


_OUT = ((6250, 128), "float32")


def kernel(x, src, dst, L0_gnn_w_ih, L0_gnn_w_hh, L0_gnn_b_ih, L0_gnn_b_hh, L0_gnn_w_lin, L0_gnn_b_lin):
    import numpy as np
    import concourse.bacc as bacc
    from concourse.bass_utils import run_bass_kernel_spmd

    x = np.ascontiguousarray(x)
    n, dim = x.shape
    tiles = -(-n // P)
    dst = np.asarray(dst).reshape(n, -1)
    padded = np.zeros((tiles * P, dst.shape[1]), dst.dtype)
    padded[:n] = dst
    steps = np.ascontiguousarray(padded.reshape(tiles, P, -1).transpose(2, 1, 0))

    def reorder(a):
        i, f, g, o = np.split(np.asarray(a), 4, axis=0)
        return np.concatenate([f, i, o, g], axis=0)

    arrays = {
        "x": x,
        "steps": steps,
        "w_ih_t": np.ascontiguousarray(reorder(L0_gnn_w_ih).T),
        "w_hh_t": np.ascontiguousarray(reorder(L0_gnn_w_hh).T),
        "b_ih": reorder(L0_gnn_b_ih),
        "b_hh": reorder(L0_gnn_b_hh),
        "w_lin_t": np.ascontiguousarray(np.asarray(L0_gnn_w_lin).T),
        "b_lin": np.ascontiguousarray(L0_gnn_b_lin),
    }
    nc = bacc.Bacc("TRN2", target_bir_lowering=False, num_devices=1)
    args = [nc.dram_tensor(k, a.shape, mybir.dt.from_np(a.dtype), kind="ExternalInput").ap()
            for k, a in arrays.items()]
    out = nc.dram_tensor("out", _OUT[0], mybir.dt.from_np(np.dtype(_OUT[1])), kind="ExternalOutput").ap()
    lstm_gnn(nc, *args, out)
    r = run_bass_kernel_spmd(nc, [arrays], core_ids=[0])
    return r.results[0]["out"]
```

```python
from contextlib import ExitStack

import concourse.bass as bass
from concourse import mybir

F32 = mybir.dt.float32
F32R = mybir.dt.float32r
I32 = mybir.dt.int32
U32 = mybir.dt.uint32
ALU = mybir.AluOpType
ACT = mybir.ActivationFunctionType

P = 128
EPS = 1e-5
FORGET, INPUT, OUTPUT, CAND = range(4)


class Batch:

    def __init__(self, groups, tail_group, n_steps, before):
        self.groups, self.tail_group, self.before = groups, tail_group, before
        self.width = len(groups)
        self.full_width = sum(g != tail_group for g in groups)
        self.body = 2 * self.width
        self.passes = n_steps // 2
        past = [(b.width, b.full_width) for b in before]
        self.unit0 = n_steps * sum(w for w, _ in past)
        self.full0 = n_steps * sum(f for _, f in past)
        self.recurrent0 = (n_steps - 1) * sum(w for w, _ in past)
        self.split0 = (n_steps - 1) * sum(f for _, f in past)

    def group(self, k):
        return self.groups[k % self.width]

    def is_tail(self, k):
        return self.group(k) == self.tail_group

    def first_step(self, i, k):
        return isinstance(i, int) and i == 0 and k < self.width

    def last_step(self, i, k):
        return isinstance(i, int) and i == self.passes - 1 and k >= self.width

    def _full(self, k):
        return self.full_width * (k // self.width) + sum(g != self.tail_group for g in self.groups[:k % self.width])

    def units(self, i, k):
        return self.unit0 + self.body * i + k

    def fulls(self, i, k):
        return self.full0 + 2 * self.full_width * i + self._full(k)

    def recurrents(self, i, k):
        return self.recurrent0 + self.body * i + k - self.width

    def splits(self, i, k):
        return self.split0 + 2 * self.full_width * i + self._full(k)


def lstm_gnn(nc, x, steps, w_ih_t, w_hh_t, b_ih, b_hh, w_lin_t, b_lin, out):
    n_nodes, dim = x.shape
    n_steps, _, n_tiles = steps.shape
    hid = w_hh_t.shape[0]
    gates = 4 * hid
    assert dim == P and hid == P and n_tiles == -(-n_nodes // P)
    full_tiles = n_nodes // P
    tail = n_nodes - full_tiles * P
    assert tail > 0 and full_tiles % 4 == 0 and n_steps % 2 == 0 and n_steps >= 6

    TPG = 4
    W = TPG * P
    BIG = full_tiles // TPG
    GROUPS = BIG + 1
    SLOTS = 6
    half = BIG // 2
    first_half = Batch(list(range(half)), BIG, n_steps, [])
    mid = half + half // 2
    second_half = Batch([*range(half, mid), BIG, *range(mid, BIG)], BIG, n_steps, [first_half])
    batches = [first_half, second_half]
    for b in batches:
        assert 2 * b.full_width % SLOTS == 0 and b.full0 % SLOTS == 0 and b.unit0 % 2 == 0
        assert not b.is_tail(0) and not b.is_tail(b.body - 1)
    FIRST = half * TPG
    assert half == SLOTS and mid < BIG and BIG == 2 * half
    n_units = n_steps * GROUPS

    table = nc.dram_tensor("gate_table", (n_nodes, gates), F32, kind="Internal").ap()

    with ExitStack() as ctx:
        def sb(name, shape, dt=F32):
            return ctx.enter_context(nc.sbuf_tensor(name, shape, dt))

        def sem(name):
            return ctx.enter_context(nc.semaphore(name))

        x_sb = sb("x_sb", [P, n_tiles, dim])
        ident = sb("ident", [P, P])
        w_ih_sb = sb("w_ih_sb", [P, gates])
        w_hh_sb = sb("w_hh_sb", [P, gates])
        w_hh_hi = sb("w_hh_hi", [P, gates], F32R)
        w_hh_lo = sb("w_hh_lo", [P, gates], F32R)
        w_lin_sb = sb("w_lin_sb", [P, dim])
        bias2 = sb("bias2", [2, gates])
        ones2 = sb("ones2", [2, P])
        b_lin_row = sb("b_lin_row", [1, dim])
        bias_all = sb("bias_all", [P, gates])
        b_lin_all = sb("b_lin_all", [P, dim])
        bias_cols = sb("bias_cols", [P, 4])
        stats = sb("stats", [P, n_tiles + FIRST, 6])
        moments = sb("moments", [P, n_tiles + FIRST, 2])
        var_eps, root, inv_root, newton, scale, shift = (
            sb(name, [P, n_tiles + FIRST]) for name in ("var_eps", "root", "inv_root", "newton", "scale", "shift"))
        normed = sb("normed", [P, 2, dim])
        feat = sb("feat", [P, 2, P])
        step_idx = sb("step_idx", [P, 2, n_tiles], I32)
        rows = sb("rows", [P, SLOTS, TPG, gates])
        table_rows = rows[:, 0, :, :]
        tail_rows = sb("tail_rows", [P, 2, gates])
        cell = sb("cell", [P, GROUPS + 2, W])
        first_x = cell[:, half:BIG, :].rearrange("p g (j d) -> p (g j) d", d=dim)
        h_hi = sb("h_hi", [P, BIG, W], F32R)
        h_lo = sb("h_lo", [P, BIG, W], F32R)
        sig = sb("sig", [P, 2, 3, W])
        prod = sb("prod", [P, 2, 2, W])
        first_feat = prod[:, :, 0, :]
        tanh_c = sb("tanh_c", [P, 2, W])
        h_full = sb("h_full", [P, 2, W])
        h_tail = sb("h_tail", [P, tail])
        ps = ctx.enter_context(nc.psum_tensor("ps", [P, 8, 512], F32))

        x_loaded = [sem(f"x_loaded{k}") for k in range(6)]
        w_ih_loaded = sem("w_ih_loaded")
        weights_loaded = sem("weights_loaded")
        biases_loaded = sem("biases_loaded")
        idx_loaded = [sem(f"idx_loaded{s}") for s in range(2)]
        ones_set = sem("ones_set")
        ident_set = sem("ident_set")
        bias_summed = sem("bias_summed")
        bias_copied = sem("bias_copied")
        stats_done = sem("stats_done")
        moments_done = sem("moments_done")
        root_step = sem("root_step")
        sqrt_done = sem("sqrt_done")
        scales_ready = sem("scales_ready")
        w_split = sem("w_split")
        tile_normed = sem("tile_normed")
        tile_transposed = sem("tile_transposed")
        feat_ready = sem("feat_ready")
        table_summed = sem("table_summed")
        table_row_ready = sem("table_row_ready")
        table_stored = [sem(f"table_stored{k}") for k in range(4)]
        residual_ready = sem("residual_ready")
        first_landed = [sem(f"first_landed{k}") for k in range(2)]
        first_normed = sem("first_normed")
        first_transposed = sem("first_transposed")
        first_feat_ready = sem("first_feat_ready")
        rows_landed = [sem(f"rows_landed{k}") for k in range(SLOTS)]
        tail_landed = [sem(f"tail_landed{s}") for s in range(2)]
        rows_used = sem("rows_used")
        tail_used = sem("tail_used")
        gathers_cleared = sem("gathers_cleared")
        cand_summed = sem("cand_summed")
        gates_summed = sem("gates_summed")
        cand_active = sem("cand_active")
        gates_active = sem("gates_active")
        products_done = sem("products_done")
        cell_ready = sem("cell_ready")
        tanh_c_ready = sem("tanh_c_ready")
        h_computed = sem("h_computed")
        h_hi_ready = sem("h_hi_ready")
        h_lo_ready = sem("h_lo_ready")
        projected = sem("projected")
        out_ready = sem("out_ready")
        out_stored = sem("out_stored")

        def width(g):
            return W if g < BIG else tail

        def wait_from_one(eng, s, value):
            if not isinstance(value, int) or value > 0:
                eng.wait_ge(s, value)

        def passes(eng, body):
            for b in batches:
                body(b, 0)
                with eng.Fori(1, b.passes - 1) as i:
                    body(b, i)
                body(b, b.passes - 1)

        def next_unit(b, i, k):
            if k + 1 < b.body:
                return b, i, k + 1
            if not (isinstance(i, int) and i == b.passes - 1):
                return b, i + 1, 0
            return (batches[1], 0, 0) if b is batches[0] else None

        def split_before(b, i, k):
            if k == 0:
                return None if isinstance(i, int) and i == 0 else (b, i - 1, b.body - 1)
            return None if b.is_tail(k - 1) or b.last_step(i, k - 1) else (b, i, k - 1)

        bounds = [0, 4, 12, 24, 36, full_tiles]
        chunks = list(zip(bounds, bounds[1:]))
        CHUNK = FIRST // 2
        stat_chunks = chunks + [(n_tiles - 1, n_tiles - 1 + CHUNK), (n_tiles - 1 + CHUNK, n_tiles - 1 + FIRST)]

        def columns(c):
            t0, t1 = stat_chunks[c]
            return slice(t0 + 1 if c else 0, t1 + 1)

        START = {2: 0, 3: 9, 4: 18, 5: 26, 6: 37}
        ROOT_OPS = 6
        assert all(START[c] + 8 < chunks[c][0] - 2 for c in (3, 4)) and full_tiles == 48

        block = ctx.enter_context(nc.Block())

        @block.sync
        def _(sp):
            xv = x[0:full_tiles * P, :].rearrange("(n p) d -> p n d", p=P)
            for c, (t0, t1) in enumerate(chunks):
                sp.dma_start(x_sb[:, t0:t1, :], xv[:, t0:t1, :]).then_inc(x_loaded[c], 16)
                if c == 0:
                    sp.dma_start(step_idx[:, 0, :], steps[0:1, :, :].rearrange("a p n -> p (a n)")
                                 ).then_inc(idx_loaded[0], 16)
                    sp.dma_start(x_sb[0:tail, full_tiles, :], x[full_tiles * P:n_nodes, :]
                                 ).then_inc(x_loaded[len(chunks)], 16)
            sp.dma_start(w_hh_sb[:, :], w_hh_t).then_inc(weights_loaded, 16)
            sp.dma_start(w_lin_sb[:, :], w_lin_t).then_inc(weights_loaded, 16)

            def store_tile(t, k, n):
                sp.wait_ge(table_row_ready, t + 1)
                sp.dma_start(table[bass.ds(t * P, n), :], table_rows[0:n, k, :]).then_inc(table_stored[k], 16)

            with sp.Fori(0, full_tiles // 4) as c:
                for k in range(4):
                    store_tile(4 * c + k, k, P)
            store_tile(full_tiles, 0, tail)

            def load_steps(b, i):
                for s in range(2):
                    if isinstance(i, int) and i == 0 and s == 0 and not b.before:
                        continue
                    wait_from_one(sp, rows_used, b.fulls(i, b.width * s) - b.full_width)
                    if b.tail_group in b.groups:
                        wait_from_one(sp, tail_used, 2 * i + s - 1)
                    t = 2 * i + s
                    sp.dma_start(step_idx[:, s, :], steps[bass.ds(t, 1), :, :].rearrange("a p n -> p (a n)")
                                 ).then_inc(idx_loaded[s], 16)

            passes(sp, load_steps)

            for g in range(GROUPS):
                sp.wait_ge(out_ready, g + 1)
                n0, t0 = g * W, g * TPG
                if g < BIG:
                    sp.dma_start(out[n0:n0 + W, :].rearrange("(n p) d -> p n d", p=P), x_sb[:, t0:t0 + TPG, :]
                                 ).then_inc(out_stored, 16)
                else:
                    sp.dma_start(out[n0:n_nodes, :], x_sb[0:tail, full_tiles, :]).then_inc(out_stored, 16)
            sp.wait_ge(out_stored, 16 * GROUPS)

        @block.gpsimd
        def _(pool):
            pool.memset(ident[:, :], 0.0).then_inc(ident_set, 1)
            pool.wait_ge(ident_set, 1)
            pool.affine_select(out=ident[:, :], in_=ident[:, :], compare_op=ALU.not_equal, fill=1.0,
                               base=0, pattern=[[-1, P]], channel_multiplier=1).then_inc(ident_set, 1)
            pool.wait_ge(idx_loaded[0], 16)
            pool.sem_inc(gathers_cleared, 1)
            for f in range(FIRST):
                pool.indirect_dma_start(
                    first_x[:, f, :], None, x,
                    bass.IndirectOffsetOnAxis(ap=step_idx[:, 0, f:f + 1].bitcast(U32), axis=0),
                ).then_inc(first_landed[f // CHUNK], 16)
            for f in range(FIRST):
                if f % CHUNK == 0:
                    pool.wait_ge(scales_ready, len(chunks) + f // CHUNK + 1)
                col = n_tiles + f
                nc.gpsimd.tensor_scalar(first_x[:, f, :], first_x[:, f, :], scale[:, col:col + 1],
                                        shift[:, col:col + 1], ALU.mult, ALU.add).then_inc(first_normed, 1)
            for k in range(4):
                pool.wait_ge(table_stored[k], 16 * len(range(k, n_tiles, 4)))

            def gather(b, i):
                for k in range(b.body):
                    g, s = b.group(k), k // b.width
                    if not b.before and b.first_step(i, k):
                        continue
                    if k % b.width == 0:
                        pool.wait_ge(idx_loaded[s], 16 * (b.passes * len(b.before) + i + 1))
                        pool.sem_inc(gathers_cleared, 1)
                    if b.is_tail(k):
                        wait_from_one(pool, tail_used, 2 * i + s - 1)
                        pool.sem_inc(gathers_cleared, 1)
                        pool.indirect_dma_start(
                            tail_rows[0:tail, s, :], None, table,
                            bass.IndirectOffsetOnAxis(
                                ap=step_idx[0:tail, s, full_tiles:full_tiles + 1].bitcast(U32), axis=0),
                        ).then_inc(tail_landed[s], 16)
                        continue
                    slot = b.fulls(0, k) % SLOTS
                    if b.before or not isinstance(i, int) or i > 0:
                        pool.wait_ge(rows_used, b.fulls(i, k) - SLOTS + 1)
                    pool.sem_inc(gathers_cleared, 1)
                    for j in range(TPG):
                        pool.indirect_dma_start(
                            rows[:, slot, j, :], None, table,
                            bass.IndirectOffsetOnAxis(
                                ap=step_idx[:, s, g * TPG + j:g * TPG + j + 1].bitcast(U32), axis=0),
                        ).then_inc(rows_landed[slot], 16)

            passes(pool, gather)

        @block.tensor
        def _(pe):
            pe.wait_ge(ones_set, 1)
            pe.wait_ge(biases_loaded, 48)
            nc.tensor.matmul(ps[:, 0, :], ones2[:, :], bias2[:, :], start=True, stop=True)
            nc.tensor.matmul(ps[:, 1, 0:dim], ones2[0:1, :], b_lin_row[:, :], start=True, stop=True)

            def transpose_tile(t, b, n):
                pe.wait_ge(tile_normed, t + 1)
                wait_from_one(pe, feat_ready, t - 1)
                nc.tensor.transpose(ps[:, 2 + b, 0:n], normed[0:n, b, :], ident[0:n, 0:n]
                                    ).then_inc(tile_transposed, 1)

            def table_tile(t, k, n):
                pe.wait_ge(feat_ready, t + 1)
                wait_from_one(pe, table_row_ready, t - 3)
                nc.tensor.matmul(ps[0:n, 4 + k, :], feat[:, k % 2, 0:n], w_ih_sb[:, :], start=True, stop=True
                                 ).then_inc(table_summed, 1)

            def four_tiles(c):
                last = isinstance(c, int) and c == full_tiles // 4 - 1
                for k in range(4):
                    transpose_tile(4 * c + k + 1, (k + 1) % 2, tail if last and k == 3 else P)
                    table_tile(4 * c + k, k, P)

            pe.wait_ge(ident_set, 2)
            transpose_tile(0, 0, P)
            for q in range(4):
                last = nc.tensor.matmul(ps[:, 1, dim + q:dim + q + 1], bias2[:, q * hid:(q + 1) * hid],
                                        ones2[:, 0:1], start=False, stop=True, skip_group_check=True)
            last.then_inc(bias_summed, 1)
            pe.wait_ge(w_ih_loaded, 16)
            four_tiles(0)
            with pe.Fori(1, full_tiles // 4 - 1) as c:
                four_tiles(c)
            four_tiles(full_tiles // 4 - 1)
            table_tile(full_tiles, 0, tail)

            def transpose_first(k):
                pe.wait_ge(first_normed, TPG * (k + 1))
                if k == 0:
                    pe.wait_ge(bias_copied, 1)
                elif k == 1:
                    pe.wait_ge(table_row_ready, n_tiles)
                else:
                    pe.wait_ge(first_feat_ready, k - 1)
                for j in range(TPG):
                    last = nc.tensor.transpose(ps[:, 4 * (k % 2) + FORGET, j * P:(j + 1) * P],
                                               first_x[:, TPG * k + j, :], ident[:, :])
                last.then_inc(first_transposed, 1)

            def first_products(k):
                base = 4 * (k % 2)
                pe.wait_ge(first_feat_ready, k + 1)
                if k == 0:
                    pe.wait_ge(feat_ready, n_tiles)
                wait_from_one(pe, cand_active, k - 1)
                nc.tensor.matmul(ps[:, base + CAND, :], w_ih_sb[:, CAND * hid:(CAND + 1) * hid],
                                 first_feat[:, k % 2, :], start=True, stop=True).then_inc(cand_summed, 1)
                wait_from_one(pe, gates_active, k - 1)
                for q in (INPUT, OUTPUT):
                    last = nc.tensor.matmul(ps[:, base + q, :], w_ih_sb[:, q * hid:(q + 1) * hid],
                                            first_feat[:, k % 2, :], start=True, stop=True)
                last.then_inc(rows_used, 1)

            def gate_sums(b, i):
                for k in range(b.body):
                    if not b.before and b.first_step(i, k):
                        continue
                    g, s = b.group(k), k // b.width
                    is_tail, first_step = b.is_tail(k), b.first_step(i, k)
                    base, n = 4 * (k % 2), width(g)
                    unit = b.units(i, k)
                    wait_from_one(pe, cand_active, unit - 1)
                    slot = b.fulls(0, k) % SLOTS
                    if is_tail:
                        pe.wait_ge(tail_landed[s], 16 * (i + 1))
                        tiles = [(tail_rows[0:tail, s, :], tail)]
                    else:
                        uses = b.full0 // SLOTS + 2 * b.full_width // SLOTS * i + (b.fulls(0, k) - b.full0) // SLOTS
                        pe.wait_ge(rows_landed[slot], 16 * TPG * uses)
                        tiles = [(rows[:, slot, j, :], P) for j in range(TPG)]
                    for q in (CAND, INPUT, OUTPUT, FORGET):
                        if q == INPUT:
                            wait_from_one(pe, gates_active, unit - 1)
                        if q == FORGET and first_step:
                            continue
                        for j, (src, m) in enumerate(tiles):
                            last = nc.tensor.matmul(ps[:, base + q, j * P:j * P + m], src[:, q * hid:(q + 1) * hid],
                                                    ident[0:m, 0:m], start=(j == 0), stop=first_step,
                                                    is_transpose=True, skip_group_check=True)
                        if first_step and q == CAND:
                            last.then_inc(cand_summed, 1)
                    last.then_inc(tail_used if is_tail else rows_used, 1)
                    if first_step:
                        continue
                    if is_tail:
                        pe.wait_ge(h_computed, unit - b.width + 1)
                        for q in (CAND, FORGET, INPUT, OUTPUT):
                            last = nc.tensor.matmul(ps[:, base + q, 0:n], w_hh_sb[:, q * hid:(q + 1) * hid],
                                                    h_tail[:, :], start=False, stop=True, skip_group_check=True)
                            if q == CAND:
                                last.then_inc(cand_summed, 1)
                        last.then_inc(gates_summed, 1)
                        continue
                    pe.wait_ge(h_lo_ready, b.splits(i, k) - b.full_width + 1)
                    for q in (CAND, FORGET, INPUT, OUTPUT):
                        acc = ps[:, base + q, 0:n]
                        hi = w_hh_hi[:, q * hid:(q + 1) * hid]
                        lo = w_hh_lo[:, q * hid:(q + 1) * hid]
                        nc.tensor.matmul(acc, hi, h_hi[:, g, 0:n], start=False, stop=False, skip_group_check=True)
                        nc.tensor.matmul(acc, hi, h_lo[:, g, 0:n], start=False, stop=False, skip_group_check=True)
                        last = nc.tensor.matmul(acc, lo, h_hi[:, g, 0:n], start=False, stop=True,
                                                skip_group_check=True)
                        if q == CAND:
                            last.then_inc(cand_summed, 1)
                    last.then_inc(gates_summed, 1)

            transpose_first(0)
            for k in range(half):
                if k + 1 < half:
                    transpose_first(k + 1)
                first_products(k)
            pe.wait_ge(w_split, 2)
            passes(pe, gate_sums)

            for g in range(GROUPS):
                pe.wait_ge(gates_active, n_units - 1 if g < 4 else n_units)
                b = first_half if g < half else second_half
                pe.wait_ge(h_computed, b.units(b.passes - 1, b.width + b.groups.index(g)) + 1)
                wait_from_one(pe, out_ready, g - 7)
                for j in range(TPG if g < BIG else 1):
                    m = P if g < BIG else tail
                    last = nc.tensor.matmul(ps[0:m, g % 8, j * dim:(j + 1) * dim], cell[:, g, j * P:j * P + m],
                                            w_lin_sb[:, :], start=(j == 0), stop=True, skip_group_check=True)
                last.then_inc(projected, 1)

        @block.scalar
        def _(act):
            act.dma_start(w_ih_sb[:, :], w_ih_t).then_inc(w_ih_loaded, 16)
            act.dma_start(bias2[0:1, :], b_ih.rearrange("(a n) -> a n", a=1)).then_inc(biases_loaded, 16)
            act.dma_start(bias2[1:2, :], b_hh.rearrange("(a n) -> a n", a=1)).then_inc(biases_loaded, 16)
            act.dma_start(b_lin_row[:, :], b_lin.rearrange("(a n) -> a n", a=1)).then_inc(biases_loaded, 16)

            def take_roots(chunk):
                cols = columns(chunk)
                act.wait_ge(root_step, ROOT_OPS * chunk + 1)
                nc.scalar.activation(root[:, cols], var_eps[:, cols], ACT.Sqrt).then_inc(sqrt_done, 1)

            def norm_tile(t, b, n, chunk):
                act.wait_ge(scales_ready, chunk + 1)
                wait_from_one(act, tile_transposed, t - 1)
                col = 0 if n == tail else t + 1
                nc.scalar.activation(normed[0:n, b, :], x_sb[0:n, bass.ds(t, 1), :].rearrange("p a d -> p (a d)"),
                                     ACT.Identity, bias=shift[0:n, bass.ds(col, 1)],
                                     scale=scale[0:n, bass.ds(col, 1)]).then_inc(tile_normed, 1)

            def relu_tile(t, b, n):
                act.wait_ge(tile_transposed, t + 1)
                nc.scalar.activation(feat[:, b, 0:n], ps[:, 2 + b, 0:n], ACT.Relu).then_inc(feat_ready, 1)

            take_roots(0)
            for t in range(2):
                norm_tile(t, t, P, 0)
            roots_at = {1: 1} | {START[c] + 8: c for c in START}
            for t in range(full_tiles):
                relu_tile(t, t % 2, P)
                if t + 2 < full_tiles:
                    norm_tile(t + 2, t % 2, P, max(c for c, (t0, _) in enumerate(chunks) if t0 <= t + 2))
                elif t + 2 == full_tiles:
                    norm_tile(t + 2, t % 2, tail, 0)
                if t in roots_at:
                    take_roots(roots_at[t])
            relu_tile(full_tiles, 0, tail)

            def activate_first(k):
                base = 4 * (k % 2)
                act.wait_ge(cand_summed, k + 1)
                wait_from_one(act, products_done, k - 1)
                nc.scalar.activation(cell[:, GROUPS + k % 2, :], ps[:, base + CAND, :], ACT.Tanh,
                                     bias=bias_cols[:, CAND:CAND + 1]).then_inc(cand_active, 1)
                act.wait_ge(rows_used, k + 1)
                wait_from_one(act, h_computed, k - 1)
                for q in (INPUT, OUTPUT):
                    last = nc.scalar.activation(sig[:, k % 2, q, :], ps[:, base + q, :], ACT.Sigmoid,
                                                bias=bias_cols[:, q:q + 1])
                last.then_inc(gates_active, 1)

            def activate_gates(b, i, k):
                if not b.before and b.first_step(i, k):
                    activate_first(k)
                    return
                buf, n, unit = k % 2, width(b.group(k)), b.units(i, k)
                base = 4 * buf
                act.wait_ge(cand_summed, unit + 1)
                wait_from_one(act, products_done, unit - 1)
                nc.scalar.activation(cell[:, GROUPS + buf, 0:n], ps[:, base + CAND, 0:n], ACT.Tanh
                                     ).then_inc(cand_active, 1)
                if not b.first_step(i, k):
                    act.wait_ge(gates_summed, b.recurrents(i, k) + 1)
                elif b.is_tail(k):
                    act.wait_ge(tail_used, 1)
                else:
                    act.wait_ge(rows_used, b.fulls(i, k) + 1)
                wait_from_one(act, h_computed, unit - 1)
                q0 = INPUT if b.first_step(i, k) else FORGET
                nc.scalar.activation(sig[:, buf, q0:CAND, 0:n], ps[:, base + q0:base + CAND, 0:n], ACT.Sigmoid
                                     ).then_inc(gates_active, 1)

            def tanh_cell(b, i, k):
                g, n = b.group(k), width(b.group(k))
                if b.first_step(i, k):
                    act.wait_ge(products_done, b.units(i, k) + 1)
                else:
                    act.wait_ge(cell_ready, b.recurrents(i, k) + 1)
                nc.scalar.activation(tanh_c[:, k % 2, 0:n], cell[:, g, 0:n], ACT.Tanh).then_inc(tanh_c_ready, 1)

            def round_h(b, i, k):
                act.wait_ge(h_computed, b.units(i, k) + 1)
                nc.scalar.activation(h_hi[:, b.group(k), :], h_full[:, b.fulls(0, k) % 2, :], ACT.Copy
                                     ).then_inc(h_hi_ready, 1)

            def activations(b, i):
                if isinstance(i, int) and i == 0 and not b.before:
                    activate_gates(b, 0, 0)
                for k in range(b.body):
                    if following := next_unit(b, i, k):
                        activate_gates(*following)
                    tanh_cell(b, i, k)
                    if split := split_before(b, i, k):
                        round_h(*split)

            passes(act, activations)

        @block.vector
        def _(dve):
            nc.vector.memset(ones2[:, :], 1.0).then_inc(ones_set, 1)
            nc.vector.memset(moments[:, :, :], 1.0).then_inc(moments_done, 1)
            dve.wait_ge(moments_done, 1)

            def row_stats(t, col, n):
                nc.vector.bn_stats(stats[0:n, bass.ds(col, 1), :].rearrange("p a s -> p (a s)"),
                                   x_sb[0:n, bass.ds(t, 1), :].rearrange("p a d -> p (a d)")
                                   ).then_inc(stats_done, 1)

            def row_moments(col, n, taken):
                dve.wait_ge(stats_done, taken)
                nc.vector.bn_aggr(moments[0:n, bass.ds(col, 1), :].rearrange("p a s -> p (a s)"),
                                  stats[0:n, bass.ds(col, 1), :].rearrange("p a s -> p (a s)")
                                  ).then_inc(moments_done, 1)

            def root_op(op, chunk):
                cols = columns(chunk)
                if op == 0:
                    dve.wait_ge(moments_done, 1 + cols.stop)
                else:
                    dve.wait_ge(root_step, ROOT_OPS * chunk + op)
                if op == 0:
                    nc.vector.tensor_scalar(var_eps[:, cols], moments[:, cols, 1], EPS, None, ALU.add
                                            ).then_inc(root_step, 1)
                elif op == 1:
                    dve.wait_ge(sqrt_done, chunk + 1)
                    nc.vector.reciprocal(inv_root[:, cols], root[:, cols]).then_inc(root_step, 1)
                elif op == 2:
                    nc.vector.tensor_tensor(newton[:, cols], inv_root[:, cols], inv_root[:, cols], ALU.mult
                                            ).then_inc(root_step, 1)
                elif op == 3:
                    nc.vector.tensor_tensor(root[:, cols], newton[:, cols], var_eps[:, cols], ALU.mult
                                            ).then_inc(root_step, 1)
                elif op == 4:
                    nc.vector.tensor_scalar(newton[:, cols], root[:, cols], -0.5, 1.5, ALU.mult, ALU.add
                                            ).then_inc(root_step, 1)
                elif op == 5:
                    nc.vector.tensor_tensor(scale[:, cols], inv_root[:, cols], newton[:, cols], ALU.mult
                                            ).then_inc(root_step, 1)
                else:
                    nc.vector.scalar_tensor_tensor(out=shift[:, cols], in0=moments[:, cols, 0], scalar=-1.0,
                                                   in1=scale[:, cols], op0=ALU.mult, op1=ALU.mult
                                                   ).then_inc(scales_ready, 1)

            def bias_tile(t, k, n):
                dve.wait_ge(table_summed, t + 1)
                wait_from_one(dve, table_stored[k], 4 * (t - k))
                nc.vector.tensor_tensor(table_rows[0:n, k, :], ps[0:n, 4 + k, :], bias_all[0:n, :], ALU.add
                                        ).then_inc(table_row_ready, 1)

            def gathered_stats(f):
                nc.vector.bn_stats(stats[:, n_tiles + f, :], first_x[:, f, :]).then_inc(stats_done, 1)

            dve.wait_ge(x_loaded[0], 16)
            for t in range(*chunks[0]):
                row_stats(t, t + 1, P)
            dve.wait_ge(x_loaded[len(chunks)], 16)
            row_stats(full_tiles, 0, tail)
            for t in range(*chunks[0]):
                row_moments(t + 1, P, t + 1)
            row_moments(0, tail, chunks[0][1] + 1)
            for op in range(ROOT_OPS + 1):
                root_op(op, 0)
            dve.wait_ge(x_loaded[1], 16)
            for t in range(*chunks[1]):
                row_stats(t, t + 1, P)
            for t in range(*chunks[1]):
                row_moments(t + 1, P, t + 2)
            for op in range(ROOT_OPS + 1):
                root_op(op, 1)
            dve.wait_ge(bias_summed, 1)
            nc.vector.tensor_copy(bias_all[:, :], ps[:, 0, :])
            nc.vector.tensor_copy(bias_cols[:, :], ps[:, 1, dim:dim + 4])
            nc.vector.tensor_copy(b_lin_all[:, :], ps[:, 1, 0:dim]).then_inc(bias_copied, 1)
            dve.wait_ge(bias_copied, 1)

            for t in range(full_tiles):
                pair, after = [], {}
                for c, start in START.items():
                    t0, t1 = stat_chunks[c]
                    if t == start:
                        dve.wait_ge(x_loaded[c] if c < len(chunks) else first_landed[c - len(chunks)],
                                    16 if c < len(chunks) else 16 * CHUNK)
                    if start <= t < start + (t1 - t0) // 2:
                        pair = [t0 + 2 * (t - start) + e for e in range(2)]
                    after |= {start + 5: (0, c), start + 7: (1, c), start + 8: (3, c)}
                for u in pair:
                    if u < full_tiles:
                        row_stats(u, u + 1, P)
                    else:
                        gathered_stats(u + 1 - n_tiles)
                bias_tile(t, t % 4, P)
                for u in pair:
                    row_moments(u + 1, P, u + 2)
                if t in after:
                    first_op, c = after[t]
                    for op in {0: (0,), 1: (1, 2), 3: (3, 4, 5, 6)}[first_op]:
                        root_op(op, c)
            bias_tile(full_tiles, 0, tail)

            def add_b_lin(g):
                blin = b_lin_all[:, :].rearrange("p (a d) -> p a d", a=1)
                tiles, m = (slice(g * TPG, g * TPG + TPG), P) if g < BIG else (slice(full_tiles, n_tiles), tail)
                count = tiles.stop - tiles.start
                nc.vector.tensor_tensor(x_sb[0:m, tiles, :], x_sb[0:m, tiles, :],
                                        blin[0:m].to_broadcast([m, count, dim]), ALU.add
                                        ).then_inc(residual_ready, 1)

            def relu_first(k):
                dve.wait_ge(first_transposed, k + 1)
                nc.vector.tensor_scalar(first_feat[:, k % 2, :], ps[:, 4 * (k % 2) + FORGET, :], 0.0, None, ALU.max
                                        ).then_inc(first_feat_ready, 1)

            relu_first(0)
            relu_first(1)
            dve.wait_ge(weights_loaded, 32)
            nc.vector.tensor_copy(w_hh_hi[:, :], w_hh_sb[:, :]).then_inc(w_split, 1)
            dve.wait_ge(w_split, 1)
            nc.vector.tensor_tensor(w_hh_lo[:, :], w_hh_sb[:, :], w_hh_hi[:, :].bitcast(F32), ALU.subtract
                                    ).then_inc(w_split, 1)

            def products(b, i, k):
                g, buf, n = b.group(k), k % 2, width(b.group(k))
                dve.wait_ge(gates_active, b.units(i, k) + 1)
                if b.first_step(i, k):
                    nc.vector.tensor_tensor(cell[:, g, 0:n], sig[:, buf, INPUT, 0:n], cell[:, GROUPS + buf, 0:n],
                                            ALU.mult).then_inc(products_done, 1)
                else:
                    after_first = isinstance(i, int) and i == 0 and k == b.width
                    wait_from_one(dve, cell_ready, b.recurrents(i, k) - (0 if after_first else 1))
                    pair = cell[:, g:GROUPS + buf + 1:GROUPS + buf - g, 0:n]
                    nc.vector.tensor_tensor(prod[:, buf, :, 0:n], sig[:, buf, FORGET:INPUT + 1, 0:n], pair, ALU.mult
                                            ).then_inc(products_done, 1)

            def new_cell(b, i, k):
                g, buf, n = b.group(k), k % 2, width(b.group(k))
                dve.wait_ge(products_done, b.units(i, k) + 1)
                nc.vector.tensor_tensor(cell[:, g, 0:n], prod[:, buf, 0, 0:n], prod[:, buf, 1, 0:n], ALU.add
                                        ).then_inc(cell_ready, 1)

            def new_h(b, i, k):
                g, buf, n = b.group(k), k % 2, width(b.group(k))
                dve.wait_ge(tanh_c_ready, b.units(i, k) + 1)
                if b.last_step(i, k):
                    dst = cell[:, g, 0:n]
                elif b.is_tail(k):
                    dst = h_tail[:, :]
                else:
                    wait_from_one(dve, h_lo_ready, b.splits(i, k) - 1)
                    dst = h_full[:, b.fulls(0, k) % 2, :]
                nc.vector.tensor_tensor(dst, sig[:, buf, OUTPUT, 0:n], tanh_c[:, buf, 0:n], ALU.mult
                                        ).then_inc(h_computed, 1)

            def low_h(b, i, k):
                g = b.group(k)
                dve.wait_ge(h_hi_ready, b.splits(i, k) + 1)
                nc.vector.tensor_tensor(h_lo[:, g, :], h_full[:, b.fulls(0, k) % 2, :], h_hi[:, g, :].bitcast(F32),
                                        ALU.subtract).then_inc(h_lo_ready, 1)

            def updates(b, i):
                first_pass = isinstance(i, int) and i == 0 and not b.before
                if first_pass:
                    products(b, 0, 0)
                for k in range(b.body):
                    if first_pass and k + 2 < half:
                        relu_first(k + 2)
                    following = next_unit(b, i, k)
                    if following:
                        products(*following)
                    new_h(b, i, k)
                    if following and not following[0].first_step(*following[1:]):
                        new_cell(*following)
                    if split := split_before(b, i, k):
                        low_h(*split)
                    if first_pass:
                        add_b_lin(k)
                if first_pass:
                    add_b_lin(BIG)

            passes(dve, updates)

            dve.wait_ge(residual_ready, GROUPS)
            for g in range(GROUPS):
                dve.wait_ge(projected, g + 1)
                tiles = slice(g * TPG, g * TPG + TPG) if g < BIG else slice(full_tiles, n_tiles)
                m, c = (P, TPG) if g < BIG else (tail, 1)
                nc.vector.tensor_tensor(x_sb[0:m, tiles, :],
                                        ps[0:m, g % 8, 0:c * dim].rearrange("p (a d) -> p a d", a=c),
                                        x_sb[0:m, tiles, :], ALU.add).then_inc(out_ready, 1)


_OUT = ((6250, 128), "float32")


def kernel(x, src, dst, L0_gnn_w_ih, L0_gnn_w_hh, L0_gnn_b_ih, L0_gnn_b_hh, L0_gnn_w_lin, L0_gnn_b_lin):
    import numpy as np
    import concourse.bacc as bacc
    from concourse.bass_utils import run_bass_kernel_spmd

    x = np.ascontiguousarray(x)
    n, dim = x.shape
    tiles = -(-n // P)
    dst = np.asarray(dst).reshape(n, -1)
    padded = np.zeros((tiles * P, dst.shape[1]), dst.dtype)
    padded[:n] = dst
    steps = np.ascontiguousarray(padded.reshape(tiles, P, -1).transpose(2, 1, 0))

    def reorder(a):
        i, f, g, o = np.split(np.asarray(a), 4, axis=0)
        return np.concatenate([f, i, o, g], axis=0)

    arrays = {
        "x": x,
        "steps": steps,
        "w_ih_t": np.ascontiguousarray(reorder(L0_gnn_w_ih).T),
        "w_hh_t": np.ascontiguousarray(reorder(L0_gnn_w_hh).T),
        "b_ih": reorder(L0_gnn_b_ih),
        "b_hh": reorder(L0_gnn_b_hh),
        "w_lin_t": np.ascontiguousarray(np.asarray(L0_gnn_w_lin).T),
        "b_lin": np.ascontiguousarray(L0_gnn_b_lin),
    }
    nc = bacc.Bacc("TRN2", target_bir_lowering=False, num_devices=1)
    args = [nc.dram_tensor(k, a.shape, mybir.dt.from_np(a.dtype), kind="ExternalInput").ap()
            for k, a in arrays.items()]
    out = nc.dram_tensor("out", _OUT[0], mybir.dt.from_np(np.dtype(_OUT[1])), kind="ExternalOutput").ap()
    lstm_gnn(nc, *args, out)
    r = run_bass_kernel_spmd(nc, [arrays], core_ids=[0])
    return r.results[0]["out"]
```
